# Optimizing a Trainium2 kernel written in Bass

```python
import numpy as np
import jax
import jax.numpy as jnp

def _softmax(x, axis=-1):
    return jax.nn.softmax(x, axis=axis)

def _gelu(x):
    return jax.nn.gelu(x, approximate=True)

def _silu(x):
    return jax.nn.silu(x)

def _sigmoid(x):
    return jax.nn.sigmoid(x)

def _layernorm(x, axis=-1, eps=1e-05):
    m = jnp.mean(x, axis=axis, keepdims=True)
    v = jnp.var(x, axis=axis, keepdims=True)
    return (x - m) / jnp.sqrt(v + eps)

def _scatter_add(tgt, idx, src, axis=0):
    return tgt.at[idx].add(src)

def _segment_sum(src, seg, n):
    return jax.ops.segment_sum(src, seg, n)
kernel_name = 'mk_adj_resnorm_d2_adj_r2_f230c8'

def setup_inputs(seed: int=0):
    np.random.seed(seed)
    _w = jnp.asarray

    def _rec_inputs():
        import jax
        import jax.numpy as jnp
        _gk = jax.random.key(seed)
        x = -0.000929 + 1 * jax.random.normal(jax.random.fold_in(_gk, 1), (32, 256, 64), jnp.float32)
        _a = jax.random.bernoulli(jax.random.fold_in(_gk, 2), 0.015625, (32, 256, 256))
        _a = jnp.logical_or(_a, jnp.swapaxes(_a, -1, -2))
        _a = jnp.logical_or(_a, jnp.eye(256, dtype=bool))
        _af = _a.astype(jnp.float32)
        _af = _af * jax.random.uniform(jax.random.fold_in(_gk, 3), (32, 256, 256), jnp.float32, 0.05, 1)
        adj = _af
        _nm = jnp.ones((32, 256), dtype=bool)
        nodemask = jnp.where(_nm, 1.0, 0.0).astype(jnp.float32)
        return (x, adj, nodemask)
    x, adj, nodemask = _rec_inputs()

    def _L0_gnn_setup():
        import jax, jax.numpy as jnp
        import numpy as np
        NORM = 1.0

        def _glorot(key, shape):
            fan_in, fan_out = shape
            lim = float(np.sqrt(6.0 / (fan_in + fan_out)))
            return jax.random.uniform(key, shape, jnp.float32, -lim, lim)

        def _gcn_layer(h, adj, W, b):
            msg = h @ W + b
            agg = jnp.einsum('bij,bjd->bid', adj, msg) / NORM
            return jax.nn.relu(agg)
        key = jax.random.key(seed)
        ks = jax.random.split(key, 12)
        B, N = (8, 1024)
        latent, hidden, out_dim = (64, 128, 64)
        inp = {'latent_features': jax.random.normal(ks[0], (B, N, latent), jnp.float32), 'adjacency_matrix': jax.random.uniform(ks[1], (B, N, N), jnp.float32), 'node_mask': jnp.ones((B, N, 1), jnp.float32), 'W0': _glorot(ks[2], (latent, hidden)), 'b0': jnp.zeros((hidden,), jnp.float32), 'W1': _glorot(ks[3], (hidden, hidden)), 'b1': jnp.zeros((hidden,), jnp.float32), 'W2': _glorot(ks[4], (hidden, hidden)), 'b2': jnp.zeros((hidden,), jnp.float32), 'Wout': _glorot(ks[5], (hidden, out_dim)), 'bout': jnp.zeros((out_dim,), jnp.float32)}
        return inp
    _L0_gnn_all = _L0_gnn_setup()
    _L0_gnn_in = {k: v for k, v in _L0_gnn_all.items() if k in ('W0', 'b0', 'W1', 'b1', 'W2', 'b2', 'Wout', 'bout')}
    del _L0_gnn_all

    def _L1_gnn_setup():
        import jax, jax.numpy as jnp
        import numpy as np
        B, N, DIN, DOUT = (8, 128, 64, 64)
        AVG_D_LOG = 4.86
        EPS = 1e-05
        NEG_BIG = 1000000000.0
        N_AGG, N_SCALE = (4, 3)

        def _pna_forward(x, adj, W_pre, b_pre, W_post, b_post):
            n = adj.shape[1]
            h_i = jnp.broadcast_to(x[:, :, None, :], (x.shape[0], n, n, x.shape[-1]))
            h_j = jnp.broadcast_to(x[:, None, :, :], (x.shape[0], n, n, x.shape[-1]))
            h_cat = jnp.concatenate([h_i, h_j], axis=-1)
            h_mod = jnp.einsum('bnme,ed->bnmd', h_cat, W_pre) + b_pre
            deg = adj.sum(-1)
            deg_safe = jnp.maximum(deg, 1.0)[..., None]
            mask = (adj > 0)[..., None]
            s1 = jnp.einsum('bnm,bnmd->bnd', adj, h_mod)
            mean = s1 / deg_safe
            s2 = jnp.einsum('bnm,bnmd->bnd', adj, h_mod * h_mod)
            var = jax.nn.relu(s2 / deg_safe - mean * mean)
            std = jnp.sqrt(var + EPS)
            mx = jnp.max(jnp.where(mask, h_mod, -NEG_BIG), axis=2)
            mn = jnp.min(jnp.where(mask, h_mod, NEG_BIG), axis=2)
            m = jnp.concatenate([mean, mx, mn, std], axis=-1)
            log_deg = jnp.log(deg + 1.0)[..., None]
            amp = m * (log_deg / AVG_D_LOG)
            att = m * (AVG_D_LOG / jnp.maximum(log_deg, EPS))
            m_all = jnp.concatenate([m, amp, att], axis=-1)
            m_cat = jnp.concatenate([x, m_all], axis=-1)
            return jnp.einsum('bne,ed->bnd', m_cat, W_post) + b_post
        key = jax.random.key(seed)
        k1, k2, k3, k4, k5, k6 = jax.random.split(key, 6)
        inp = jax.random.normal(k1, (B, N, DIN), dtype=jnp.float32)
        adj = jax.random.randint(k2, (B, N, N), 0, 2).astype(jnp.float32)
        W_pre = jax.random.normal(k3, (2 * DIN, DIN), dtype=jnp.float32) / np.sqrt(2 * DIN)
        b_pre = jnp.zeros((DIN,), dtype=jnp.float32)
        post_in = (N_AGG * N_SCALE + 1) * DIN
        W_post = jax.random.normal(k4, (post_in, DOUT), dtype=jnp.float32) / np.sqrt(post_in)
        b_post = jnp.zeros((DOUT,), dtype=jnp.float32)
        return {'input': inp, 'adj': adj, 'W_pre': W_pre, 'b_pre': b_pre, 'W_post': W_post, 'b_post': b_post}
    _L1_gnn_all = _L1_gnn_setup()
    _L1_gnn_in = {k: v for k, v in _L1_gnn_all.items() if k in ('W_pre', 'b_pre', 'W_post', 'b_post')}
    del _L1_gnn_all
    return {'x': x, 'adj': adj, 'nodemask': nodemask, 'L0_gnn_W0': _L0_gnn_in['W0'], 'L0_gnn_b0': _L0_gnn_in['b0'], 'L0_gnn_W1': _L0_gnn_in['W1'], 'L0_gnn_b1': _L0_gnn_in['b1'], 'L0_gnn_W2': _L0_gnn_in['W2'], 'L0_gnn_b2': _L0_gnn_in['b2'], 'L0_gnn_Wout': _L0_gnn_in['Wout'], 'L0_gnn_bout': _L0_gnn_in['bout'], 'L1_gnn_W_pre': _L1_gnn_in['W_pre'], 'L1_gnn_b_pre': _L1_gnn_in['b_pre'], 'L1_gnn_W_post': _L1_gnn_in['W_post'], 'L1_gnn_b_post': _L1_gnn_in['b_post']}

def reference(x, adj, nodemask, L0_gnn_W0, L0_gnn_b0, L0_gnn_W1, L0_gnn_b1, L0_gnn_W2, L0_gnn_b2, L0_gnn_Wout, L0_gnn_bout, L1_gnn_W_pre, L1_gnn_b_pre, L1_gnn_W_post, L1_gnn_b_post):
    import jax
    import jax.numpy as jnp

    def _L0_gnn_ref(latent_features, adjacency_matrix, node_mask, W0, b0, W1, b1, W2, b2, Wout, bout):
        import jax, jax.numpy as jnp
        import numpy as np
        NORM = 1.0

        def _glorot(key, shape):
            fan_in, fan_out = shape
            lim = float(np.sqrt(6.0 / (fan_in + fan_out)))
            return jax.random.uniform(key, shape, jnp.float32, -lim, lim)

        def _gcn_layer(h, adj, W, b):
            msg = h @ W + b
            agg = jnp.einsum('bij,bjd->bid', adj, msg) / NORM
            return jax.nn.relu(agg)
        h = _gcn_layer(latent_features, adjacency_matrix, W0, b0)
        h = _gcn_layer(h, adjacency_matrix, W1, b1)
        h = _gcn_layer(h, adjacency_matrix, W2, b2)
        return (h @ Wout + bout) * node_mask

    def _L1_gnn_ref(input, adj, W_pre, b_pre, W_post, b_post):
        import jax, jax.numpy as jnp
        import numpy as np
        B, N, DIN, DOUT = (8, 128, 64, 64)
        AVG_D_LOG = 4.86
        EPS = 1e-05
        NEG_BIG = 1000000000.0
        N_AGG, N_SCALE = (4, 3)

        def _pna_forward(x, adj, W_pre, b_pre, W_post, b_post):
            n = adj.shape[1]
            h_i = jnp.broadcast_to(x[:, :, None, :], (x.shape[0], n, n, x.shape[-1]))
            h_j = jnp.broadcast_to(x[:, None, :, :], (x.shape[0], n, n, x.shape[-1]))
            h_cat = jnp.concatenate([h_i, h_j], axis=-1)
            h_mod = jnp.einsum('bnme,ed->bnmd', h_cat, W_pre) + b_pre
            deg = adj.sum(-1)
            deg_safe = jnp.maximum(deg, 1.0)[..., None]
            mask = (adj > 0)[..., None]
            s1 = jnp.einsum('bnm,bnmd->bnd', adj, h_mod)
            mean = s1 / deg_safe
            s2 = jnp.einsum('bnm,bnmd->bnd', adj, h_mod * h_mod)
            var = jax.nn.relu(s2 / deg_safe - mean * mean)
            std = jnp.sqrt(var + EPS)
            mx = jnp.max(jnp.where(mask, h_mod, -NEG_BIG), axis=2)
            mn = jnp.min(jnp.where(mask, h_mod, NEG_BIG), axis=2)
            m = jnp.concatenate([mean, mx, mn, std], axis=-1)
            log_deg = jnp.log(deg + 1.0)[..., None]
            amp = m * (log_deg / AVG_D_LOG)
            att = m * (AVG_D_LOG / jnp.maximum(log_deg, EPS))
            m_all = jnp.concatenate([m, amp, att], axis=-1)
            m_cat = jnp.concatenate([x, m_all], axis=-1)
            return jnp.einsum('bne,ed->bnd', m_cat, W_post) + b_post
        return _pna_forward(input, adj, W_pre, b_pre, W_post, b_post)
    x = _layernorm(x + _L0_gnn_ref(x, adj, nodemask[..., None], L0_gnn_W0, L0_gnn_b0, L0_gnn_W1, L0_gnn_b1, L0_gnn_W2, L0_gnn_b2, L0_gnn_Wout, L0_gnn_bout), axis=-1)
    x = _layernorm(x + _L1_gnn_ref(x, adj, L1_gnn_W_pre, L1_gnn_b_pre, L1_gnn_W_post, L1_gnn_b_post), axis=-1)
    return x

_drawn_inputs = setup_inputs


def setup_inputs(seed=0):
    import zlib

    import numpy as np

    out = dict(_drawn_inputs(seed))
    spreads = {'L0_gnn_b0': (0.0, 0.1),
     'L0_gnn_b1': (0.0, 0.1),
     'L0_gnn_b2': (0.0, 0.1),
     'L0_gnn_bout': (0.0, 0.699),
     'L1_gnn_b_pre': (0.0, 0.1),
     'L1_gnn_b_post': (0.0, 0.1)}
    factors = {}
    for name, (base, spread) in spreads.items():
        noise = np.random.default_rng([zlib.crc32(name.encode()), seed]).standard_normal(out[name].shape)
        drawn = base * np.exp(spread * noise) if base else spread * noise
        out[name] = jnp.asarray(drawn.astype(out[name].dtype))
    for name, factor in factors.items():
        out[name] = (out[name] * factor).astype(out[name].dtype)
    return out
```

```python
import concourse.bass as bass
from concourse import mybir
from contextlib import ExitStack


def gcn_pna_program(nc, x, adj, nodemask, W0, b0, W1, b1, W2, b2, Wout, bout,
                    W_pre, b_pre, W_post, b_post, out):
    f32, f16, bf16, i32 = mybir.dt.float32, mybir.dt.float16, mybir.dt.bfloat16, mybir.dt.int32
    ALU = mybir.AluOpType
    ACT = mybir.ActivationFunctionType
    AX = mybir.AxisListType.X

    B, N, D = x.shape
    H = W0.shape[1]
    P = 128
    NH = N // P
    PAIRS = 7
    SLOTS = 2 * PAIRS
    ROUNDS = -(-P // (2 * SLOTS)) * 2
    RANK0 = 1024
    HALF = 0.5
    LO = 2.0 ** 14
    BIG = 1e9
    XNORM = 8.01
    AVG_D_LOG = 4.86
    EPS = 1e-5
    assert NH == 2 and D == 64 and H == P

    adj_v = adj.rearrange("b (h p) m -> p (b h) m", p=P)
    x_v = x.rearrange("b (h p) d -> p (b h) d", p=P)
    out_v = out.rearrange("b (h p) d -> p (b h) d", p=P)
    mask_v = nodemask.rearrange("b (h p) -> (b h) p", p=P)

    ctx = ExitStack()
    with ctx:
        def sb(name, shape, dt=f32):
            return ctx.enter_context(nc.sbuf_tensor(name, shape, dt))

        def pb(name, shape):
            return ctx.enter_context(nc.psum_tensor(name, shape, f32))

        def sem(name):
            return ctx.enter_context(nc.semaphore(name))

        ident = sb("ident", [P, P])
        W0b = sb("W0b", [D + 1, H])
        W1s, W2s = sb("W1s", [H, H]), sb("W2s", [H, H])
        Wouts = sb("Wouts", [H, D])
        boutr = sb("boutr", [P, D])
        Wuv = sb("Wuv", [D + 2, 4, D])
        Wum = sb("Wum", [D + 2, 2, D])
        Wst = sb("Wst", [P, 3, D])
        Wmx = sb("Wmx", [P, 3, D])
        Wx = sb("Wx", [D + 2, D])
        tri = sb("tri", [P, P], f16)
        ones = sb("ones", [P, 1], f16)
        ones64 = sb("ones64", [D, P])
        Wsq = sb("Wsq", [D, D])
        shift0 = sb("shift0", [P, D])
        shift = sb("shift", [P, D])
        brow = sb("brow", [D + 1, 2, H])
        epscol = sb("epscol", [P, 1])
        gate = sb("gate", [1, 1])
        lo_scale = sb("lo_scale", [P, 2 * D])
        maskrows = sb("maskrows", [NH * B, P])
        nmask = sb("nmask", [P, NH * B])

        adjn = sb("adjn", [P, 2, NH, N])
        adjT = sb("adjT", [P, 2, NH, N])
        maskT = sb("maskT", [P, NH, N], f16)
        xa = sb("xa", [P, 2, NH, D + 1])
        aggT = sb("aggT", [D + 1, N])
        hT = sb("hT", [H, N])
        msg = sb("msg", [P, NH, H])
        yb = sb("yb", [P, NH, D])
        y = sb("y", [P, NH, D])
        st1 = sb("st1", [P, NH, 6])
        mv1 = sb("mv1", [P, NH, 2])
        sd1 = sb("sd1", [P, NH])
        rs1 = sb("rs1", [P, NH])
        x1 = sb("x1", [P, 2, NH, P])
        x1T = sb("x1T", [D + 2, 2, N])
        code = sb("code", [P, 2, NH, N], f16)
        most = sb("most", [P, NH, NH])
        total = sb("total", [P, NH])

        vhi = sb("vhi", [P, NH, 2 * D], f16)
        vres = sb("vres", [P, NH, 2 * D])
        vlo = sb("vlo", [P, NH, 2 * D], f16)
        us = sb("us", [P, NH, D])
        vv = sb("vv", [P, NH, 2 * D + 1])
        onehot = sb("onehot", [P, PAIRS, NH, 2, N], f16)
        best = sb("best", [P, NH, 2, N])
        best2 = sb("best2", [P, 2, N])
        best1 = sb("best1", [P, N])
        deg = sb("deg", [P, NH])
        degs = sb("degs", [P, NH])
        rdeg = sb("rdeg", [P, NH])
        ratio = sb("ratio", [P, NH])
        slack = sb("slack", [P, NH])
        lg = sb("lg", [P, NH])
        lgs = sb("lgs", [P, NH])
        amp = sb("amp", [P, NH])
        att = sb("att", [P, NH])
        att0 = sb("att0", [P, NH])
        q = sb("q", [P, NH, 2 * D])
        ms = sb("ms", [P, NH, 2 * D])
        q1sq = sb("q1sq", [P, NH, D])
        vb = sb("vb", [P, NH, D])
        cs = sb("cs", [P, NH, D])
        uc = sb("uc", [P, NH, D])
        var0 = sb("var0", [P, NH, D])
        var1 = sb("var1", [P, NH, D])
        msT = sb("msT", [P, N])
        mx = sb("mx", [P, N])
        za = sb("za", [P, NH, D])
        zb = sb("zb", [P, NH, D])
        z = sb("z", [P, NH, D])
        st2 = sb("st2", [P, NH, 6])
        mv2 = sb("mv2", [P, NH, 2])
        sd2 = sb("sd2", [P, NH])
        rs2 = sb("rs2", [P, NH])
        zo = sb("zo", [P, 2, NH, D])

        worst = sb("worst", [P, 1])
        over = sb("over", [P, 1], f16)
        flag = sb("flag", [1, 1], i32)
        back = sb("back", [P, ROUNDS])
        keep = sb("keep", [P, ROUNDS])
        carry = sb("carry", [P, N])

        pT = pb("pT", [P, 512])
        pG = pb("pG", [P, 512])
        pC = pb("pC", [P, 512])
        pU = pb("pU", [P, 512])
        pS = [pb(f"pS{i}", [P, 1024]) for i in range(2)]
        pU_uv = pU[:, 0:NH * 4 * D].rearrange("p (h c) -> p h c", h=NH)
        pU_s = pU[:, 0:NH * (2 * D + 1)].rearrange("p (h c) -> p h c", h=NH)
        pC_y = pC[:, 0:NH * 3 * D].rearrange("p (h c) -> p h c", h=NH)

        consts_set = sem("consts_set")
        mask_loaded_t = sem("mask_loaded_t")
        mask_turned = sem("mask_turned")
        nmask_ready = sem("nmask_ready")
        wpost_neg = sem("wpost_neg")
        wpre_neg = sem("wpre_neg")
        adj_turned = sem("adj_turned")
        adjT_copied = sem("adjT_copied")
        maskT_ready = sem("maskT_ready")
        agg0_done = sem("agg0_done")
        aggT_copied = sem("aggT_copied")
        nums_done = sem("nums_done")
        counts_done = sem("counts_done")
        h1_done = sem("h1_done")
        h1_relu = sem("h1_relu")
        msg1_done = sem("msg1_done")
        msg1_ready = sem("msg1_ready")
        h2_done = sem("h2_done")
        h2_relu = sem("h2_relu")
        msg2_done = sem("msg2_done")
        msg2_ready = sem("msg2_ready")
        h3_done = sem("h3_done")
        h3_relu = sem("h3_relu")
        wsq_ready = sem("wsq_ready")
        wsq_summed = sem("wsq_summed")
        shift0_ready = sem("shift0_ready")
        shift_ready = sem("shift_ready")
        wrows_ready = sem("wrows_ready")
        yout_done = sem("yout_done")
        yb_ready = sem("yb_ready")
        ym_ready = sem("ym_ready")
        y_ready = sem("y_ready")
        st1_ready = sem("st1_ready")
        mv1_ready = sem("mv1_ready")
        sd1_ready = sem("sd1_ready")
        rs1_ready = sem("rs1_ready")
        x1_ready = sem("x1_ready")
        x1_turned = sem("x1_turned")
        x1T_copied = sem("x1T_copied")
        code_ready = sem("code_ready")
        total_ready = sem("total_ready")
        most_ready = sem("most_ready")
        iso_ready = sem("iso_ready")
        uv_done = sem("uv_done")
        vhi_ready = sem("vhi_ready")
        vres_ready = sem("vres_ready")
        vlo_ready = sem("vlo_ready")
        u_copied = sem("u_copied")
        v_copied = sem("v_copied")
        vsq_ready = sem("vsq_ready")
        onehot_ready = sem("onehot_ready")
        slot_done = sem("slot_done")
        best_started = sem("best_started")
        best_updated = sem("best_updated")
        best2_ready = sem("best2_ready")
        best1_ready = sem("best1_ready")
        sums_done = sem("sums_done")
        deg_copied = sem("deg_copied")
        lg_ready = sem("lg_ready")
        degs_ready = sem("degs_ready")
        rdeg_ready = sem("rdeg_ready")
        ratio_ready = sem("ratio_ready")
        slack_ready = sem("slack_ready")
        lgs_ready = sem("lgs_ready")
        amp_ready = sem("amp_ready")
        att0_ready = sem("att0_ready")
        att_ready = sem("att_ready")
        q_ready = sem("q_ready")
        mean_ready = sem("mean_ready")
        q1sq_ready = sem("q1sq_ready")
        vb_ready = sem("vb_ready")
        cs_ready = sem("cs_ready")
        uc_ready = sem("uc_ready")
        var0_ready = sem("var0_ready")
        var1_ready = sem("var1_ready")
        std_ready = sem("std_ready")
        ms_turned = sem("ms_turned")
        msT_copied = sem("msT_copied")
        mx_ready = sem("mx_ready")
        post_done = sem("post_done")
        za_ready = sem("za_ready")
        zb_ready = sem("zb_ready")
        z_ready = sem("z_ready")
        st2_ready = sem("st2_ready")
        mv2_ready = sem("mv2_ready")
        sd2_ready = sem("sd2_ready")
        rs2_ready = sem("rs2_ready")
        zo_ready = sem("zo_ready")
        worst_ready = sem("worst_ready")
        over_ready = sem("over_ready")
        over_summed = sem("over_summed")
        flag_ready = sem("flag_ready")
        rounds_set = sem("rounds_set")
        carry_ready = sem("carry_ready")
        w_loaded = sem("w_loaded")
        adj_loaded = [sem("adj_loaded0"), sem("adj_loaded1")]
        x_loaded = [sem("x_loaded0"), sem("x_loaded1")]
        out_stored = [sem("out_stored0"), sem("out_stored1")]
        N_W_ALL = 32
        N_CONST = 11
        poolstep = sem("poolstep")

        def past(count):
            return max(count, 0) if isinstance(count, int) else count

        def over_flag(eng):
            eng.wait_ge(flag_ready, 1)
            return nc.values_load(flag[0:1, 0:1], engines=[eng.engine], min_val=0, max_val=P)

        def every_round(eng, one_round, at_end=None):
            with eng.If(over_flag(eng) > 0):
                with eng.Fori(0, B) as b:
                    with eng.Fori(0, ROUNDS // 2) as pair:
                        k = B // 2 + b * (ROUNDS // 2) + pair
                        for par in range(2):
                            one_round(2 * k + par, par, k, b, 2 * pair + par)
                if at_end:
                    at_end()

        block = ctx.enter_context(nc.Block())

        def every_turn(eng, stage_a, stage_b, stage_c, turn, flag_step=None):
            def graph(b):
                return b, b % 2, b // 2

            stage_a(*graph(0))
            stage_a(*graph(1))
            stage_b(*graph(0))
            for b in (1, 2):
                turn(graph(b + 1), graph(b), graph(b - 1))
            with eng.Fori(1, B // 2 - 1) as i:
                turn((2 * i + 2, 0, i + 1), (2 * i + 1, 1, i), (2 * i, 0, i))
                turn((2 * i + 3, 1, i + 1), (2 * i + 2, 0, i + 1), (2 * i + 1, 1, i))
            if flag_step:
                flag_step()
            stage_c(*graph(B - 2))
            stage_b(*graph(B - 1))
            stage_c(*graph(B - 1))

        @block.sync
        def _(sp):
            def w(dst, src):
                sp.dma_start(dst, src).then_inc(w_loaded, 16)

            def load(b, par, k, graph=None):
                graph = b if graph is None else graph
                sp.wait_ge(adj_turned, past(b - 1))
                sp.dma_start(adjn[:, par, :, :], adj_v[:, bass.ds(2 * graph, 2), :]).then_inc(adj_loaded[par], 16)
                sp.wait_ge(y_ready, past(b - 1))
                sp.dma_start(xa[:, par, :, 0:D], x_v[:, bass.ds(2 * graph, 2), :]).then_inc(x_loaded[par], 16)

            load(0, 0, 0)
            load(1, 1, 0)
            w(W0b[0:D, :], W0)
            w(W0b[D:D + 1, :], b0[None, :])
            w(W1s[:, :], W1)
            w(W2s[:, :], W2)
            w(Wouts[:, :], Wout)
            w(brow[D:D + 1, 0, :], b1[None, :])
            w(brow[D:D + 1, 1, :], b2[None, :])
            w(boutr[:, :], bout[None, :].to_broadcast([P, D]))
            w(maskrows[:, :], mask_v)
            w(Wuv[0:D, 0, :], W_pre[0:D, :])
            w(Wuv[0:D, 1, :], W_pre[D:2 * D, :])
            w(Wuv[0:D, 2, :], W_pre[D:2 * D, :])
            w(Wuv[0:D, 3, :], W_pre[D:2 * D, :])
            w(Wum[0:D, 0, :], W_pre[0:D, :])
            w(Wum[0:D, 1, :], W_pre[0:D, :])
            w(Wx[0:D, :], W_post[0:D, :])
            for c in range(3):
                r = D + 4 * D * c
                w(Wst[0:D, c, :], W_post[r:r + D, :])
                w(Wmx[0:D, c, :], W_post[r + D:r + 2 * D, :])
                w(Wmx[D:P, c, :], W_post[r + 2 * D:r + 3 * D, :])
                w(Wst[D:P, c, :], W_post[r + 3 * D:r + 4 * D, :])
            sp.wait_ge(poolstep, 5)
            w(Wuv[D:D + 1, 0, :], b_pre[None, :])
            w(Wum[D:D + 1, 0, :], b_pre[None, :])
            w(Wum[D:D + 1, 1, :], b_pre[None, :])
            w(Wx[D:D + 1, :], b_post[None, :])
            with sp.Fori(0, B // 2 - 1) as i:
                load(2 * i + 2, 0, i + 1)
                load(2 * i + 3, 1, i + 1)

            def all_stored(graphs):
                for par in range(2):
                    sp.wait_ge(out_stored[par], 16 * (graphs // 2))

            all_stored(B)
            every_round(sp, lambda v, par, k, graph, r: load(v, par, k, graph),
                        lambda: all_stored(B + B * ROUNDS))

        @block.tensor
        def _(pe):
            mm = nc.tensor.matmul

            pe.wait_ge(w_loaded, 16 * N_W_ALL)
            pe.wait_ge(consts_set, N_CONST)
            nc.tensor.transpose(pT[0:P, 0:NH * B], maskrows[:, :], ident[0:NH * B, 0:NH * B])\
                .then_inc(mask_turned, 1)
            pe.wait_ge(nmask_ready, 1)
            pe.wait_ge(wsq_ready, 1)
            mm(pU[:, 0:D], ones64[:, :], Wsq[:, :], start=True, stop=True).then_inc(wsq_summed, 1)
            pe.wait_ge(wpost_neg, 1)
            pe.wait_ge(wrows_ready, 4)

            def turn_adj(b, par, k):
                pe.wait_ge(adj_loaded[par], 16 * (k + 1))
                pe.wait_ge(adjT_copied, past(b))
                pe.wait_ge(total_ready, past(b))
                pe.wait_ge(most_ready, past(b))
                for mh in range(NH):
                    for nh in range(NH):
                        o = (mh * NH + nh) * P
                        ins = nc.tensor.transpose(pT[:, o:o + P], adjn[:, par, nh, mh * P:(mh + 1) * P], ident[:, :])
                ins.then_inc(adj_turned, 1)

            def agg0(b, par, k):
                pe.wait_ge(x_loaded[par], 16 * (k + 1))
                pe.wait_ge(adjT_copied, b + 1)
                pe.wait_ge(x1T_copied, past(b))
                for mh in range(NH):
                    ins = mm(pG[0:D + 1, 0:N], xa[:, par, mh, :], adjT[:, par, mh, :], start=(mh == 0), stop=(mh == 1))
                ins.then_inc(agg0_done, 1)

            def h1(b):
                pe.wait_ge(aggT_copied, b + 1)
                mm(pG[:, 0:N], W0b[:, :], aggT[:, :], start=True, stop=True).then_inc(h1_done, 1)

            def msg_mm(b, h_relu, W, done):
                pe.wait_ge(h_relu, b + 1)
                for nh in range(NH):
                    ins = mm(pG[:, nh * H:(nh + 1) * H], hT[:, nh * P:(nh + 1) * P], W[:, :], start=True, stop=True)
                ins.then_inc(done, 1)

            def agg_mm(b, par, msg_ready, layer, done):
                pe.wait_ge(msg_ready, b + 1)
                mm(pG[:, 0:N], brow[D:D + 1, layer, :], aggT[D:D + 1, :], start=True, stop=False)
                for mh in range(NH):
                    ins = mm(pG[:, 0:N], msg[:, mh, :], adjT[:, par, mh, :], start=False, stop=(mh == 1))
                ins.then_inc(done, 1)

            def number(b):
                pe.wait_ge(maskT_ready, b + 1)
                pe.wait_ge(z_ready, past(b - 1))
                for h in range(NH):
                    ins = mm(pC[:, h * N:(h + 1) * N], tri[:, :], maskT[:, h, :], start=True, stop=True)
                ins.then_inc(nums_done, 1)
                for nh in range(NH):
                    for mh in range(NH):
                        o = nh * NH + mh
                        ins = mm(pT[:, o:o + 1], maskT[:, mh, nh * P:(nh + 1) * P], ones[:, :], start=True, stop=True)
                ins.then_inc(counts_done, 1)

            def out_mm(b):
                pe.wait_ge(h3_relu, b + 1)
                for nh in range(NH):
                    ins = mm(pG[:, nh * D:(nh + 1) * D], hT[:, nh * P:(nh + 1) * P], Wouts[:, :], start=True, stop=True)
                ins.then_inc(yout_done, 1)

            def turn_x1(b, par):
                pe.wait_ge(x1_ready, 2 * b + 2)
                pe.wait_ge(iso_ready, b + 1)
                for nh in range(NH):
                    ins = nc.tensor.transpose(pG[:, nh * P:(nh + 1) * P], x1[:, par, nh, :], ident[:, :])
                ins.then_inc(x1_turned, 1)

            def uv(b, par):
                pe.wait_ge(x1T_copied, b + 1)
                pe.wait_ge(q_ready, past(2 * b))
                pe.wait_ge(deg_copied, past(b))
                for nh in range(NH):
                    ins = mm(pU_uv[:, nh, :], x1T[:, par, nh * P:(nh + 1) * P], Wuv[:, :, :].rearrange("k a b -> k (a b)"),
                             start=True, stop=True)
                ins.then_inc(uv_done, 1)

            def slots(b, par, t):
                pe.wait_ge(onehot_ready, 2 * PAIRS * b + 2 * t + 2)
                if t == 0:
                    pe.wait_ge(vhi_ready, b + 1)
                    pe.wait_ge(vlo_ready, b + 1)
                if t == 0:
                    pe.wait_ge(best_updated, past((PAIRS - 1) * b - 1))
                elif t == 1:
                    pe.wait_ge(best_updated, past((PAIRS - 1) * b))
                elif t == 2:
                    pe.wait_ge(best_started, b + 1)
                else:
                    pe.wait_ge(best_updated, past((PAIRS - 1) * b + t - 2))
                dst = pS[(par * PAIRS + t) % 2]
                for h in range(NH):
                    o = dst[:, h * 512:(h + 1) * 512]
                    oh = onehot[:, t, h, :, :].rearrange("p j n -> p (j n)")
                    mm(o, vhi[:, h, :], oh, start=True, stop=False)
                    ins = mm(o, vlo[:, h, :], oh.bitcast(bf16), start=False, stop=True)
                ins.then_inc(slot_done, 1)

            def sums(b, par):
                pe.wait_ge(v_copied, b + 1)
                pe.wait_ge(vsq_ready, b + 1)
                pe.wait_ge(u_copied, b + 1)
                pe.wait_ge(vhi_ready, b + 1)
                pe.wait_ge(vres_ready, b + 1)
                for nh in range(NH):
                    for mh in range(NH):
                        ins = mm(pU_s[:, nh, :], adjT[:, par, mh, nh * P:(nh + 1) * P], vv[:, mh, :],
                                 start=(mh == 0), stop=(mh == 1))
                ins.then_inc(sums_done, 1)

            def turn_ms(b, par, coded=None):
                pe.wait_ge(mean_ready, 2 * b + 2)
                pe.wait_ge(std_ready, b + 1)
                pe.wait_ge(code_ready, (min(b + 2, B) if isinstance(b, int) else b + 2) if coded is None else coded)
                pe.wait_ge(z_ready, past(b))
                for nh in range(NH):
                    nc.tensor.transpose(pC[:, nh * P:(nh + 1) * P], ms[:, nh, :], ident[:, :])
                mm(pC[:, N:2 * N], Wum[:, :, :].rearrange("k a b -> k (a b)"), x1T[:, par, :], start=True, stop=True)\
                    .then_inc(ms_turned, 1)

            def post(b, par):
                pe.wait_ge(msT_copied, b + 1)
                pe.wait_ge(mx_ready, b + 1)
                for nh in range(NH):
                    n = slice(nh * P, (nh + 1) * P)
                    mm(pC_y[:, nh, :], msT[:, n], Wst[:, :, :].rearrange("k a b -> k (a b)"), start=True, stop=False)
                    mm(pC_y[:, nh, 0:D], x1T[:, par, n], Wx[:, :], start=False, stop=False, skip_group_check=True)
                    ins = mm(pC_y[:, nh, :], mx[:, n], Wmx[:, :, :].rearrange("k a b -> k (a b)"), start=False, stop=True)
                ins.then_inc(post_done, 1)

            def stage_a(b, par, k):
                turn_adj(b, par, k)
                agg0(b, par, k)
                h1(b)
                msg_mm(b, h1_relu, W1s, msg1_done)
                agg_mm(b, par, msg1_ready, 0, h2_done)
                msg_mm(b, h2_relu, W2s, msg2_done)
                number(b)
                agg_mm(b, par, msg2_ready, 1, h3_done)
                out_mm(b)
                turn_x1(b, par)

            def stage_b(b, par, k):
                uv(b, par)
                for t in range(PAIRS):
                    slots(b, par, t)
                    if t == 1:
                        sums(b, par)

            def stage_c(b, par, k):
                turn_ms(b, par)
                post(b, par)

            def turn(ga, gb, gc):
                (a, apar, ak), (b, bpar, _), (c, cpar, _) = ga, gb, gc
                turn_ms(c, cpar)
                turn_adj(a, apar, ak)
                uv(b, bpar)
                post(c, cpar)
                agg0(a, apar, ak)
                slots(b, bpar, 0)
                h1(a)
                slots(b, bpar, 1)
                msg_mm(a, h1_relu, W1s, msg1_done)
                sums(b, bpar)
                slots(b, bpar, 2)
                agg_mm(a, apar, msg1_ready, 0, h2_done)
                slots(b, bpar, 3)
                msg_mm(a, h2_relu, W2s, msg2_done)
                number(a)
                slots(b, bpar, 4)
                agg_mm(a, apar, msg2_ready, 1, h3_done)
                slots(b, bpar, 5)
                out_mm(a)
                slots(b, bpar, 6)
                turn_x1(a, apar)

            def sum_over():
                pe.wait_ge(over_ready, 1)
                mm(pT[0:1, 0:1], ones[:, :], over[:, :], start=True, stop=True).then_inc(over_summed, 1)

            def one_round(v, par, k, graph, r):
                stage_a(v, par, k)
                stage_b(v, par, k)
                turn_ms(v, par, coded=v + 1)
                post(v, par)

            every_turn(pe, stage_a, stage_b, stage_c, turn, sum_over)
            every_round(pe, one_round)

        @block.scalar
        def _(act):
            af = nc.scalar.activation
            act.wait_ge(w_loaded, 16 * N_W_ALL)
            act.wait_ge(consts_set, N_CONST)
            act.wait_ge(wsq_summed, 1)
            af(shift0[:, :], pU[:, 0:D], ACT.Sqrt, scale=XNORM * XNORM).then_inc(shift0_ready, 1)

            def copy_adjT(b, par):
                act.wait_ge(adj_turned, b + 1)
                act.wait_ge(sums_done, past(b - 1))
                af(adjT[:, par, :, :].rearrange("p h n -> p (h n)"), pT[:, :], ACT.Copy).then_inc(adjT_copied, 1)

            def copy_agg0(b):
                act.wait_ge(agg0_done, b + 1)
                af(aggT[:, :], pG[0:D + 1, 0:N], ACT.Copy).then_inc(aggT_copied, 1)

            def relu(b, src, dst):
                act.wait_ge(src, b + 1)
                af(hT[:, :], pG[:, 0:N], ACT.Relu).then_inc(dst, 1)

            def copy_code(b, par, r=None):
                act.wait_ge(nums_done, b + 1)
                act.wait_ge(onehot_ready, past(2 * PAIRS * (b - 1)))
                dst = code[:, par, :, :].rearrange("p h n -> p (h n)")
                if r is None:
                    af(dst, pC[:, :], ACT.Copy).then_inc(code_ready, 1)
                else:
                    af(dst, pC[:, :], ACT.Identity, bias=back[:, bass.ds(r, 1)]).then_inc(code_ready, 1)

            def copy_msg(b, src, dst):
                act.wait_ge(src, b + 1)
                af(msg[:, :, :].rearrange("p h c -> p (h c)"), pG[:, 0:N], ACT.Copy).then_inc(dst, 1)

            def sd_1(b):
                act.wait_ge(mv1_ready, 2 * b + 2)
                af(sd1[:, :], mv1[:, :, 1], ACT.Sqrt, bias=epscol[:, 0:1]).then_inc(sd1_ready, 1)

            def copy_x1T(b, par):
                act.wait_ge(x1_turned, b + 1)
                act.wait_ge(post_done, past(b - 1))
                af(x1T[:, par, :], pG[0:D + 2, 0:N], ACT.Copy).then_inc(x1T_copied, 1)

            def v_parts(b):
                act.wait_ge(uv_done, b + 1)
                act.wait_ge(slot_done, past(PAIRS * b))
                af(vhi[:, :, :], pU_uv[:, :, 2 * D:4 * D], ACT.Copy).then_inc(vhi_ready, 1)
                act.wait_ge(uc_ready, past(b))
                act.wait_ge(mean_ready, past(2 * b))
                af(us[:, :, :], pU_uv[:, :, 0:D], ACT.Copy).then_inc(u_copied, 1)
                act.wait_ge(sums_done, past(b))
                af(vv[:, :, 0:D], pU_uv[:, :, D:2 * D], ACT.Copy).then_inc(v_copied, 1)
                af(vv[:, :, D:2 * D], pU_uv[:, :, D:2 * D], ACT.Square).then_inc(vsq_ready, 1)

            def start_best(b, par):
                act.wait_ge(slot_done, PAIRS * b + 1)
                act.wait_ge(best2_ready, past(b))
                af(best[:, :, :, :].rearrange("p h j n -> p (h j n)"), pS[(par * PAIRS) % 2][:, :], ACT.Copy)\
                    .then_inc(best_started, 1)

            def log_deg(b):
                act.wait_ge(deg_copied, b + 1)
                act.wait_ge(lgs_ready, past(b))
                act.wait_ge(amp_ready, past(b))
                af(lg[:, :], deg[:, :], ACT.Ln, bias=1.0).then_inc(lg_ready, 1)

            def std(b):
                act.wait_ge(var1_ready, b + 1)
                act.wait_ge(ms_turned, past(b))
                af(ms[:, :, D:2 * D], var1[:, :, :], ACT.Sqrt).then_inc(std_ready, 1)

            def copy_msT(b):
                act.wait_ge(ms_turned, b + 1)
                act.wait_ge(post_done, past(b))
                act.wait_ge(mx_ready, b + 1)
                af(msT[:, :], pC[:, 0:N], ACT.Copy).then_inc(msT_copied, 1)

            def sd_2(b):
                act.wait_ge(mv2_ready, 2 * b + 2)
                af(sd2[:, :], mv2[:, :, 1], ACT.Sqrt, bias=epscol[:, 0:1]).then_inc(sd2_ready, 1)

            def store(b, par, k, graph=None):
                graph = b if graph is None else graph
                act.wait_ge(zo_ready, 2 * b + 2)
                act.dma_start(out_v[:, bass.ds(2 * graph, 2), :], zo[:, par, :, :]).then_inc(out_stored[par], 16)

            def stage_a(b, par, k, r=None):
                copy_adjT(b, par)
                copy_agg0(b)
                relu(b, h1_done, h1_relu)
                copy_msg(b, msg1_done, msg1_ready)
                relu(b, h2_done, h2_relu)
                copy_msg(b, msg2_done, msg2_ready)
                copy_code(b, par, r)
                relu(b, h3_done, h3_relu)
                sd_1(b)
                copy_x1T(b, par)

            def stage_b(b, par, k):
                v_parts(b)
                start_best(b, par)
                log_deg(b)
                std(b)

            def stage_c(b, par, k):
                copy_msT(b)
                sd_2(b)
                store(b, par, k)

            def turn(ga, gb, gc):
                (a, apar, _), (b, bpar, _), (c, cpar, ck) = ga, gb, gc
                copy_adjT(a, apar)
                copy_msT(c)
                v_parts(b)
                copy_agg0(a)
                start_best(b, bpar)
                relu(a, h1_done, h1_relu)
                sd_2(c)
                store(c, cpar, ck)
                copy_msg(a, msg1_done, msg1_ready)
                relu(a, h2_done, h2_relu)
                log_deg(b)
                copy_msg(a, msg2_done, msg2_ready)
                copy_code(a, apar)
                std(b)
                relu(a, h3_done, h3_relu)
                sd_1(a)
                copy_x1T(a, apar)

            def one_round(v, par, k, graph, r):
                act.wait_ge(rounds_set, ROUNDS + 3)
                stage_a(v, par, k, r)
                stage_b(v, par, k)
                copy_msT(v)
                sd_2(v)
                act.wait_ge(out_stored[1 - par], 16 * (k + par))
                store(v, par, k, graph)

            every_turn(act, stage_a, stage_b, stage_c, turn)
            every_round(act, one_round)

        @block.vector
        def _(dve):
            v = nc.vector
            v.memset(xa[:, 0, :, D:D + 1], 1.0).then_inc(consts_set, 1)
            v.memset(xa[:, 1, :, D:D + 1], 1.0).then_inc(consts_set, 1)
            v.memset(x1[:, :, :, :], 1.0).then_inc(consts_set, 1)
            v.memset(vv[:, :, 2 * D:2 * D + 1], 1.0).then_inc(consts_set, 1)
            v.memset(epscol[:, :], EPS).then_inc(consts_set, 1)
            v.memset(lo_scale[:, :], LO).then_inc(consts_set, 1)
            v.memset(most[:, :, :], 0.0).then_inc(consts_set, 1)
            v.memset(ones[:, :], 1.0).then_inc(consts_set, 1)
            v.memset(ones64[:, :], 1.0).then_inc(consts_set, 1)
            dve.wait_ge(w_loaded, 16 * N_W_ALL)
            dve.wait_ge(consts_set, N_CONST)
            v.tensor_tensor(Wsq[:, :], Wuv[0:D, 1, :], Wuv[0:D, 1, :], ALU.mult).then_inc(wsq_ready, 1)
            v.tensor_scalar(Wuv[0:D, 3, :], Wuv[0:D, 3, :], -1.0, None, ALU.mult).then_inc(wpre_neg, 1)
            v.tensor_scalar(Wum[0:D, 1, :], Wum[0:D, 1, :], -1.0, None, ALU.mult).then_inc(wpre_neg, 1)
            v.tensor_scalar(Wmx[D:P, :, :], Wmx[D:P, :, :], -1.0, None, ALU.mult).then_inc(wpost_neg, 1)
            dve.wait_ge(mask_turned, 1)
            v.tensor_copy(nmask[:, :], pT[:, 0:NH * B]).then_inc(nmask_ready, 1)
            dve.wait_ge(shift0_ready, 1)
            row = slice(D, D + 1)
            for i in range(2):
                v.tensor_copy(Wuv[row, 2 + i, :], shift0[row, :]).then_inc(wrows_ready, 1)
            v.tensor_tensor(Wum[row, 0, :], Wum[row, 0, :], shift0[row, :], ALU.subtract).then_inc(wrows_ready, 1)
            v.scalar_tensor_tensor(out=Wum[row, 1, :], in0=Wum[row, 1, :], scalar=-1.0, in1=shift0[row, :],
                                   op0=ALU.mult, op1=ALU.subtract).then_inc(wrows_ready, 1)
            dve.wait_ge(nmask_ready, 1)

            def get_mask(b, par):
                dve.wait_ge(adjT_copied, b + 1)
                dve.wait_ge(counts_done, past(b))
                v.tensor_scalar(maskT[:, :, :].rearrange("p h n -> p (h n)"),
                                adjT[:, par, :, :].rearrange("p h n -> p (h n)"), 0.0, None, ALU.is_gt)\
                    .then_inc(maskT_ready, 1)

            def count(b, par):
                dve.wait_ge(counts_done, b + 1)
                v.tensor_reduce(total[:, :], pT[:, 0:NH * NH].rearrange("p (a b) -> p a b", a=NH), AX, ALU.add)\
                    .then_inc(total_ready, 1)
                dve.wait_ge(most_ready, past(b))
                v.tensor_tensor(most[:, :, :], pT[:, 0:NH * NH].rearrange("p (a b) -> p a b", a=NH), most[:, :, :],
                                ALU.max).then_inc(most_ready, 1)
                dve.wait_ge(total_ready, b + 1)
                dve.wait_ge(x1_turned, past(b - 1))
                v.tensor_scalar(x1[:, par, :, D + 1], total[:, :], 0.0, None, ALU.is_equal).then_inc(iso_ready, 1)

            def residual(b, par, graph=None):
                graph = b if graph is None else graph
                dve.wait_ge(yout_done, b + 1)
                v.tensor_tensor(yb[:, :, :], pG[:, 0:NH * D].rearrange("p (h c) -> p h c", h=NH),
                                boutr[:, None, :].to_broadcast([P, NH, D]), ALU.add).then_inc(yb_ready, 1)
                dve.wait_ge(yb_ready, b + 1)
                for h in range(NH):
                    v.scalar_tensor_tensor(out=y[:, h, :], in0=yb[:, h, :], scalar=nmask[:, bass.ds(2 * graph + h, 1)],
                                           in1=xa[:, par, h, 0:D], op0=ALU.mult, op1=ALU.add)\
                        .then_inc(y_ready if h else ym_ready, 1)

            def stats(b, src, ready, st, st_ready, mv, mv_ready):
                for h in range(NH):
                    dve.wait_ge(ready[h], b + 1)
                    v.bn_stats(st[:, h, :], src[:, h, :]).then_inc(st_ready, 1)
                dve.wait_ge(st_ready, 2 * b + 2)
                v.memset(gate[:, :], 0.0)
                for h in range(NH):
                    v.bn_aggr(mv[:, h, :], st[:, h, :]).then_inc(mv_ready, 1)

            def norm(b, src, mv, sd, sd_ready, rs, rs_ready, dst, dst_ready):
                dve.wait_ge(sd_ready, b + 1)
                v.reciprocal(rs[:, :], sd[:, :]).then_inc(rs_ready, 1)
                dve.wait_ge(rs_ready, b + 1)
                for h in range(NH):
                    v.tensor_scalar(dst[:, h, :], src[:, h, :], mv[:, h, 0:1], rs[:, h:h + 1],
                                    ALU.subtract, ALU.mult).then_inc(dst_ready, 1)

            def norm1(b, par):
                dve.wait_ge(x1_turned, past(b - 1))
                dve.wait_ge(za_ready, past(2 * (b - 1)))
                norm(b, y, mv1, sd1, sd1_ready, rs1, rs1_ready, x1[:, par, :, 0:D], x1_ready)

            def make_onehot(b, par, t):
                dve.wait_ge(slot_done, past(PAIRS * (b - 1) + t + 1))
                dve.wait_ge(code_ready, b + 1)
                for j in range(2):
                    v.tensor_scalar(onehot[:, t, :, j, :], code[:, par, :, :], float(RANK0 + 2 * t + j + 1), HALF,
                                    ALU.is_equal, ALU.mult).then_inc(onehot_ready, 1)

            def low_part(b):
                dve.wait_ge(vhi_ready, b + 1)
                dve.wait_ge(vsq_ready, b + 1)
                dve.wait_ge(vlo_ready, past(b))
                v.tensor_tensor(vres[:, :, :], pU_uv[:, :, 2 * D:4 * D], vhi[:, :, :], ALU.subtract)\
                    .then_inc(vres_ready, 1)

            def update_best(b, par, t):
                dve.wait_ge(slot_done, PAIRS * b + t + 1)
                if t == 1:
                    dve.wait_ge(best_started, b + 1)
                else:
                    dve.wait_ge(best_updated, past((PAIRS - 1) * b + t - 1))
                bv = best[:, :, :, :].rearrange("p h j n -> p (h j n)")
                v.tensor_tensor(bv, pS[(par * PAIRS + t) % 2][:, :], bv, ALU.max).then_inc(best_updated, 1)

            def degrees(b):
                dve.wait_ge(sums_done, b + 1)
                v.tensor_copy(deg[:, :], pU_s[:, :, 2 * D]).then_inc(deg_copied, 1)
                dve.wait_ge(deg_copied, b + 1)
                v.tensor_scalar(degs[:, :], deg[:, :], 1.0, None, ALU.max).then_inc(degs_ready, 1)
                dve.wait_ge(degs_ready, b + 1)
                v.reciprocal(rdeg[:, :], degs[:, :]).then_inc(rdeg_ready, 1)
                dve.wait_ge(rdeg_ready, b + 1)
                v.tensor_tensor(ratio[:, :], deg[:, :], rdeg[:, :], ALU.mult).then_inc(ratio_ready, 1)
                dve.wait_ge(uc_ready, past(b))
                dve.wait_ge(vb_ready, past(b))
                dve.wait_ge(cs_ready, past(b))
                for h in range(NH):
                    v.tensor_scalar(q[:, h, :], pU_s[:, h, 0:2 * D], rdeg[:, h:h + 1], None, ALU.mult)\
                        .then_inc(q_ready, 1)
                dve.wait_ge(ratio_ready, b + 1)
                v.tensor_scalar(slack[:, :], ratio[:, :], -1.0, 1.0, ALU.mult, ALU.add).then_inc(slack_ready, 1)
                dve.wait_ge(u_copied, b + 1)
                dve.wait_ge(ms_turned, past(b))
                for h in range(NH):
                    dve.wait_ge(q_ready, 2 * b + 1 + h)
                    v.scalar_tensor_tensor(out=ms[:, h, 0:D], in0=us[:, h, :], scalar=ratio[:, h:h + 1],
                                           in1=q[:, h, 0:D], op0=ALU.mult, op1=ALU.add).then_inc(mean_ready, 1)

            def scalers(b):
                dve.wait_ge(lg_ready, b + 1)
                dve.wait_ge(zb_ready, past(2 * b))
                v.tensor_scalar(lgs[:, :], lg[:, :], EPS, None, ALU.max).then_inc(lgs_ready, 1)
                v.tensor_scalar(amp[:, :], lg[:, :], 1.0 / AVG_D_LOG, None, ALU.mult).then_inc(amp_ready, 1)
                dve.wait_ge(lgs_ready, b + 1)
                v.reciprocal(att0[:, :], lgs[:, :]).then_inc(att0_ready, 1)
                dve.wait_ge(att0_ready, b + 1)
                v.tensor_scalar(att[:, :], att0[:, :], AVG_D_LOG, None, ALU.mult).then_inc(att_ready, 1)

            def variance(b):
                dve.wait_ge(uc_ready, b + 1)
                dve.wait_ge(vb_ready, b + 1)
                dve.wait_ge(slack_ready, b + 1)
                for h in range(NH):
                    v.scalar_tensor_tensor(out=var0[:, h, :], in0=uc[:, h, :], scalar=slack[:, h:h + 1],
                                           in1=vb[:, h, :], op0=ALU.mult, op1=ALU.add).then_inc(var0_ready, 1)
                dve.wait_ge(var0_ready, 2 * b + 2)
                dve.wait_ge(std_ready, past(b))
                v.tensor_scalar(var1[:, :, :], var0[:, :, :], 0.0, EPS, ALU.max, ALU.add).then_inc(var1_ready, 1)

            def fold_best(b):
                dve.wait_ge(best_updated, (PAIRS - 1) * (b + 1))
                v.tensor_tensor(best2[:, :, :], best[:, 0, :, :], best[:, 1, :, :], ALU.max).then_inc(best2_ready, 1)
                dve.wait_ge(best2_ready, b + 1)
                dve.wait_ge(mx_ready, past(b))
                v.tensor_tensor(best1[:, :], best2[:, 0, :], best2[:, 1, :], ALU.max).then_inc(best1_ready, 1)

            def carry_best(v, r):
                dve.wait_ge(best1_ready, v + 1)
                dve.wait_ge(mx_ready, past(v))
                nc.vector.scalar_tensor_tensor(out=carry[:, :], in0=carry[:, :], scalar=keep[:, bass.ds(r, 1)],
                                               in1=best1[:, :], op0=ALU.mult, op1=ALU.max)\
                    .then_inc(carry_ready, 1)

            def add_u(b, top=best1):
                dve.wait_ge(ms_turned, b + 1)
                dve.wait_ge(best1_ready, b + 1)
                dve.wait_ge(post_done, past(b))
                v.scalar_tensor_tensor(out=mx[:, :], in0=top[:, :], scalar=1.0 / HALF, in1=pC[:, N:2 * N],
                                       op0=ALU.mult, op1=ALU.add).then_inc(mx_ready, 1)

            def combine(b, par):
                dve.wait_ge(post_done, b + 1)
                dve.wait_ge(amp_ready, b + 1)
                dve.wait_ge(att_ready, b + 1)
                for h in range(NH):
                    v.scalar_tensor_tensor(out=za[:, h, :], in0=pC_y[:, h, D:2 * D], scalar=amp[:, h:h + 1],
                                           in1=x1[:, par, h, 0:D], op0=ALU.mult, op1=ALU.add).then_inc(za_ready, 1)
                for h in range(NH):
                    dve.wait_ge(za_ready, 2 * b + 1 + h)
                    v.scalar_tensor_tensor(out=zb[:, h, :], in0=pC_y[:, h, 2 * D:3 * D], scalar=att[:, h:h + 1],
                                           in1=za[:, h, :], op0=ALU.mult, op1=ALU.add).then_inc(zb_ready, 1)
                dve.wait_ge(zb_ready, 2 * b + 2)
                v.tensor_tensor(z[:, :, :], pC_y[:, :, 0:D], zb[:, :, :], ALU.add).then_inc(z_ready, 1)
                stats(b, z, (z_ready, z_ready), st2, st2_ready, mv2, mv2_ready)

            def norm2(b, par, k):
                dve.wait_ge(out_stored[par], past(16 * k))
                norm(b, z, mv2, sd2, sd2_ready, rs2, rs2_ready, zo[:, par, :, :], zo_ready)

            def stats1(b):
                stats(b, y, (ym_ready, y_ready), st1, st1_ready, mv1, mv1_ready)

            def stage_a(b, par, k):
                get_mask(b, par)
                count(b, par)
                residual(b, par)
                stats1(b)
                norm1(b, par)

            def stage_b(b, par, k):
                low_part(b)
                for t in range(PAIRS):
                    make_onehot(b, par, t)
                for t in range(1, PAIRS):
                    update_best(b, par, t)
                    if t == 2:
                        degrees(b)
                    if t == 3:
                        scalers(b)
                    if t == 4:
                        variance(b)
                fold_best(b)

            def stage_c(b, par, k):
                add_u(b)
                combine(b, par)
                norm2(b, par, k)

            def turn(ga, gb, gc):
                (a, apar, _), (b, bpar, _), (c, cpar, ck) = ga, gb, gc
                make_onehot(b, bpar, 0)
                add_u(c)
                low_part(b)
                make_onehot(b, bpar, 1)
                get_mask(a, apar)
                make_onehot(b, bpar, 2)
                combine(c, cpar)
                make_onehot(b, bpar, 3)
                update_best(b, bpar, 1)
                norm2(c, cpar, ck)
                degrees(b)
                update_best(b, bpar, 2)
                make_onehot(b, bpar, 4)
                scalers(b)
                update_best(b, bpar, 3)
                make_onehot(b, bpar, 5)
                variance(b)
                update_best(b, bpar, 4)
                make_onehot(b, bpar, 6)
                count(a, apar)
                update_best(b, bpar, 5)
                residual(a, apar)
                stats1(a)
                update_best(b, bpar, 6)
                norm1(a, apar)
                fold_best(b)

            def make_flag():
                dve.wait_ge(most_ready, B)
                v.tensor_reduce(worst[:, :], most[:, :, :].rearrange("p a b -> p (a b)"), AX, ALU.max)\
                    .then_inc(worst_ready, 1)
                dve.wait_ge(worst_ready, 1)
                v.tensor_scalar(over[:, :], worst[:, :], float(SLOTS), None, ALU.is_gt)\
                    .then_inc(over_ready, 1)
                dve.wait_ge(over_summed, 1)
                v.tensor_copy(flag[0:1, 0:1], pT[0:1, 0:1]).then_inc(flag_ready, 1)

            def one_round(n, par, k, graph, r):
                get_mask(n, par)
                count(n, par)
                residual(n, par, graph)
                stats1(n)
                norm1(n, par)
                stage_b(n, par, k)
                carry_best(n, r)
                dve.wait_ge(carry_ready, n - B + 1)
                add_u(n, carry)
                combine(n, par)
                norm2(n, par, k)

            every_turn(dve, stage_a, stage_b, stage_c, turn, make_flag)
            dve.wait_ge(flag_ready, 1)
            with dve.If(over_flag(dve) > 0):
                for r in range(ROUNDS):
                    v.memset(back[:, r:r + 1], float(-SLOTS * r)).then_inc(rounds_set, 1)
                v.memset(carry[:, :], 0.0).then_inc(rounds_set, 1)
                v.memset(keep[:, 0:1], 0.0).then_inc(rounds_set, 1)
                v.memset(keep[:, 1:ROUNDS], 1.0).then_inc(rounds_set, 1)
                dve.wait_ge(rounds_set, ROUNDS + 3)
            every_round(dve, one_round)

        @block.gpsimd
        def _(pool):
            g = nc.gpsimd
            cs_ = consts_set
            n = [9]

            def step(ins):
                n[0] += 1
                ins.then_inc(cs_, 1)

            g.memset(ident[:, :], 0.0).then_inc(poolstep, 1)
            g.memset(tri[:, :], 1.0).then_inc(poolstep, 1)
            pool.wait_ge(poolstep, 2)
            g.memset(Wuv[D:D + 2, :, :], 0.0).then_inc(poolstep, 1)
            pool.wait_ge(poolstep, 3)
            g.memset(Wum[D:D + 2, :, :], -BIG).then_inc(poolstep, 1)
            pool.wait_ge(poolstep, 4)
            g.memset(Wx[D:D + 2, :], 0.0).then_inc(poolstep, 1)
            pool.wait_ge(poolstep, 5)
            step(g.affine_select(out=ident[:, :], in_=ident[:, :], compare_op=ALU.not_equal, fill=1.0, base=0,
                                 pattern=[[-1, P]], channel_multiplier=1))
            g.affine_select(out=tri[:, :], in_=tri[:, :], compare_op=ALU.is_ge, fill=0.0, base=0,
                            pattern=[[1, P]], channel_multiplier=-1).then_inc(poolstep, 1)
            pool.wait_ge(poolstep, 6)
            step(g.affine_select(out=tri[:, :], in_=tri[:, :], compare_op=ALU.not_equal, fill=float(RANK0 + 1), base=0,
                                 pattern=[[-1, P]], channel_multiplier=1))
            assert n[0] == N_CONST, n

            def low(b):
                pool.wait_ge(vres_ready, b + 1)
                pool.wait_ge(slot_done, past(PAIRS * b))
                g.tensor_tensor(vlo[:, :, :], vres[:, :, :], lo_scale[:, None, :].to_broadcast([P, NH, 2 * D]), ALU.mult).then_inc(vlo_ready, 1)

            def terms(b):
                pool.wait_ge(q_ready, 2 * b + 2)
                g.tensor_tensor(q1sq[:, :, :], q[:, :, 0:D], q[:, :, 0:D], ALU.mult).then_inc(q1sq_ready, 1)
                pool.wait_ge(mean_ready, 2 * b + 2)
                g.tensor_tensor(cs[:, :, :], ms[:, :, 0:D], q[:, :, 0:D], ALU.add).then_inc(cs_ready, 1)
                pool.wait_ge(q1sq_ready, b + 1)
                pool.wait_ge(var0_ready, past(2 * b))
                g.tensor_tensor(vb[:, :, :], q[:, :, D:2 * D], q1sq[:, :, :], ALU.subtract).then_inc(vb_ready, 1)
                pool.wait_ge(cs_ready, b + 1)
                g.tensor_tensor(uc[:, :, :], us[:, :, :], cs[:, :, :], ALU.mult).then_inc(uc_ready, 1)

            for b in range(2):
                low(b)
                terms(b)
            with pool.Fori(2, B) as b:
                low(b)
                terms(b)

            def one_round(v, par, k, graph, r):
                low(v)
                terms(v)

            every_round(pool, one_round)


_INS = ['x', 'adj', 'nodemask', 'L0_gnn_W0', 'L0_gnn_b0', 'L0_gnn_W1', 'L0_gnn_b1', 'L0_gnn_W2', 'L0_gnn_b2',
        'L0_gnn_Wout', 'L0_gnn_bout', 'L1_gnn_W_pre', 'L1_gnn_b_pre', 'L1_gnn_W_post', 'L1_gnn_b_post']


def kernel(**inputs):
    import numpy as _np
    import concourse.bacc as _bacc
    from concourse import mybir as _mybir
    from concourse.bass_utils import run_bass_kernel_spmd as _run

    nc = _bacc.Bacc("TRN2", target_bir_lowering=False, num_devices=1)
    arrays, args = {}, []
    for name in _INS:
        a = _np.ascontiguousarray(inputs[name])
        arrays[f"in_{name}_dram"] = a
        args.append(nc.dram_tensor(f"in_{name}_dram", a.shape, _mybir.dt.from_np(a.dtype), kind="ExternalInput").ap())
    shape = _np.asarray(inputs["x"]).shape
    args.append(nc.dram_tensor("out_dram", shape, _mybir.dt.float32, kind="ExternalOutput").ap())
    gcn_pna_program(nc, *args)
    r = _run(nc, [arrays], core_ids=[0])
    return r.results[0]["out_dram"]
```

```python
import concourse.bass as bass
from concourse import mybir
from contextlib import ExitStack


def gcn_pna_program(nc, x, adj, nodemask, W0, b0, W1, b1, W2, b2, Wout, bout,
                    W_pre, b_pre, W_post, b_post, out):
    f32, f16, bf16, i32 = mybir.dt.float32, mybir.dt.float16, mybir.dt.bfloat16, mybir.dt.int32
    ALU = mybir.AluOpType
    ACT = mybir.ActivationFunctionType
    AX = mybir.AxisListType.X

    B, N, D = x.shape
    H = W0.shape[1]
    P = 128
    NH = N // P
    PAIRS = 7
    SLOTS = 2 * PAIRS
    ROUNDS = -(-P // (2 * SLOTS)) * 2
    RANK0 = 1024
    HALF = 0.5
    LO = 2.0 ** 14
    BIG = 1e9
    XNORM = 8.01
    AVG_D_LOG = 4.86
    EPS = 1e-5
    assert NH == 2 and D == 64 and H == P

    adj_v = adj.rearrange("b (h p) m -> p (b h) m", p=P)
    x_v = x.rearrange("b (h p) d -> p (b h) d", p=P)
    out_v = out.rearrange("b (h p) d -> p (b h) d", p=P)
    mask_v = nodemask.rearrange("b (h p) -> (b h) p", p=P)

    ctx = ExitStack()
    with ctx:
        def sb(name, shape, dt=f32):
            return ctx.enter_context(nc.sbuf_tensor(name, shape, dt))

        def pb(name, shape):
            return ctx.enter_context(nc.psum_tensor(name, shape, f32))

        def sem(name):
            return ctx.enter_context(nc.semaphore(name))

        ident = sb("ident", [P, P])
        W0b = sb("W0b", [D + 1, H])
        W1s, W2s = sb("W1s", [H, H]), sb("W2s", [H, H])
        Wouts = sb("Wouts", [H, D])
        boutr = sb("boutr", [1, D])
        onerow = sb("onerow", [1, P])
        Wuv = sb("Wuv", [D + 2, 4, D])
        Wum = sb("Wum", [D + 2, 2, D])
        Wst = sb("Wst", [P, 3, D])
        Wmx = sb("Wmx", [P, 3, D])
        Wx = sb("Wx", [D + 2, D])
        tri = sb("tri", [P, P], f16)
        ones = sb("ones", [P, 1], f16)
        ones64 = sb("ones64", [D, P])
        Wsq = sb("Wsq", [D, D])
        shift0 = sb("shift0", [P, D])
        shift = sb("shift", [P, D])
        brow = sb("brow", [D + 1, 2, H])
        epscol = sb("epscol", [P, 1])
        gate = sb("gate", [1, 1])
        lo_scale = sb("lo_scale", [P, 2 * D])
        maskrows = sb("maskrows", [NH * B, P])
        nmask = sb("nmask", [P, NH * B])

        adjn = sb("adjn", [P, 2, NH, N])
        adjT = sb("adjT", [P, 2, NH, N])
        maskT = sb("maskT", [P, 2, NH, N], f16)
        xa = sb("xa", [P, 2, NH, D + 1])
        aggT = sb("aggT", [D + 1, N])
        hT = sb("hT", [H, N])
        msg = sb("msg", [P, NH, H])
        y = sb("y", [P, NH, D])
        st1 = sb("st1", [P, NH, 6])
        mv1 = sb("mv1", [P, NH, 2])
        sd1 = sb("sd1", [P, NH])
        rs1 = sb("rs1", [P, NH])
        x1 = sb("x1", [P, 2, NH, P])
        x1T = sb("x1T", [D + 2, 2, N])
        code = sb("code", [P, 2, NH, N], f16)
        most = sb("most", [P, NH, NH])
        total = sb("total", [P, NH])

        vhi = sb("vhi", [P, 2, NH, 2 * D], f16)
        vres = sb("vres", [P, NH, 2 * D])
        vlo = sb("vlo", [P, 2, NH, 2 * D], f16)
        us = sb("us", [P, NH, D])
        vv = sb("vv", [P, NH, 2 * D + 1])
        onehot = sb("onehot", [P, PAIRS, NH, 2, N], f16)
        best = sb("best", [P, NH, 2, N])
        best2 = sb("best2", [P, 2, N])
        best1 = sb("best1", [P, N])
        deg = sb("deg", [P, NH])
        degs = sb("degs", [P, NH])
        rdeg = sb("rdeg", [P, NH])
        ratio = sb("ratio", [P, NH])
        slack = sb("slack", [P, NH])
        lg = sb("lg", [P, NH])
        lgs = sb("lgs", [P, NH])
        amp = sb("amp", [P, 2, NH])
        att = sb("att", [P, 2, NH])
        att0 = sb("att0", [P, NH])
        q = sb("q", [P, NH, 2 * D])
        ms = sb("ms", [P, 2, NH, 2 * D])
        q1sq = sb("q1sq", [P, NH, D])
        vb = sb("vb", [P, NH, D])
        cs = sb("cs", [P, NH, D])
        uc = sb("uc", [P, NH, D])
        var0 = sb("var0", [P, NH, D])
        var1 = sb("var1", [P, NH, D])
        msT = sb("msT", [P, N])
        mx = sb("mx", [P, N])
        plain = sb("plain", [P, NH, D])
        za = sb("za", [P, NH, D])
        z = sb("z", [P, NH, D])
        st2 = sb("st2", [P, NH, 6])
        mv2 = sb("mv2", [P, NH, 2])
        sd2 = sb("sd2", [P, NH])
        rs2 = sb("rs2", [P, NH])
        zo = sb("zo", [P, 2, NH, D])

        worst = sb("worst", [P, 1])
        over = sb("over", [P, 1], f16)
        flag = sb("flag", [1, 1], i32)
        back = sb("back", [P, ROUNDS])
        keep = sb("keep", [P, ROUNDS])
        carry = sb("carry", [P, N])

        pT = pb("pT", [P, 512])
        pG = pb("pG", [P, 512])
        pC = pb("pC", [P, 512])
        pU = pb("pU", [P, 512])
        pS = [pb(f"pS{i}", [P, 1024]) for i in range(2)]
        pU_uv = pU[:, 0:NH * 4 * D].rearrange("p (h c) -> p h c", h=NH)
        pU_s = pU[:, 0:NH * (2 * D + 1)].rearrange("p (h c) -> p h c", h=NH)
        pC_y = pC[:, 0:NH * 3 * D].rearrange("p (h c) -> p h c", h=NH)

        consts_set = sem("consts_set")
        mask_loaded_t = sem("mask_loaded_t")
        mask_turned = sem("mask_turned")
        nmask_ready = sem("nmask_ready")
        wpost_neg = sem("wpost_neg")
        wpre_neg = sem("wpre_neg")
        adj_turned = sem("adj_turned")
        adjT_copied = sem("adjT_copied")
        maskT_ready = sem("maskT_ready")
        agg0_done = sem("agg0_done")
        aggT_copied = sem("aggT_copied")
        nums_done = sem("nums_done")
        counts_done = sem("counts_done")
        h1_done = sem("h1_done")
        h1_relu = sem("h1_relu")
        msg1_done = sem("msg1_done")
        msg1_ready = sem("msg1_ready")
        h2_done = sem("h2_done")
        h2_relu = sem("h2_relu")
        msg2_done = sem("msg2_done")
        msg2_ready = sem("msg2_ready")
        h3_done = sem("h3_done")
        h3_relu = sem("h3_relu")
        wsq_ready = sem("wsq_ready")
        wsq_summed = sem("wsq_summed")
        shift0_ready = sem("shift0_ready")
        shift_ready = sem("shift_ready")
        wrows_ready = sem("wrows_ready")
        wcopies_ready = sem("wcopies_ready")
        rows_filled = sem("rows_filled")
        yout_done = sem("yout_done")
        y_ready = sem("y_ready")
        st1_ready = sem("st1_ready")
        mv1_ready = sem("mv1_ready")
        sd1_ready = sem("sd1_ready")
        rs1_ready = sem("rs1_ready")
        x1_ready = sem("x1_ready")
        x1_turned = sem("x1_turned")
        x1T_copied = sem("x1T_copied")
        code_ready = sem("code_ready")
        total_ready = sem("total_ready")
        most_ready = sem("most_ready")
        iso_ready = sem("iso_ready")
        uv_done = sem("uv_done")
        vhi_ready = sem("vhi_ready")
        vres_ready = sem("vres_ready")
        vlo_ready = sem("vlo_ready")
        u_copied = sem("u_copied")
        v_copied = sem("v_copied")
        vsq_ready = sem("vsq_ready")
        onehot_ready = sem("onehot_ready")
        slot_done = sem("slot_done")
        best_started = sem("best_started")
        best_updated = sem("best_updated")
        best2_ready = sem("best2_ready")
        wx_ready = sem("wx_ready")
        best1_ready = sem("best1_ready")
        sums_done = sem("sums_done")
        deg_copied = sem("deg_copied")
        lg_ready = sem("lg_ready")
        degs_ready = sem("degs_ready")
        rdeg_ready = sem("rdeg_ready")
        ratio_ready = sem("ratio_ready")
        slack_ready = sem("slack_ready")
        lgs_ready = sem("lgs_ready")
        amp_ready = sem("amp_ready")
        att0_ready = sem("att0_ready")
        att_ready = sem("att_ready")
        q_ready = sem("q_ready")
        mean_ready = sem("mean_ready")
        q1sq_ready = sem("q1sq_ready")
        vb_ready = sem("vb_ready")
        cs_ready = sem("cs_ready")
        uc_ready = sem("uc_ready")
        var0_ready = sem("var0_ready")
        var1_ready = sem("var1_ready")
        std_ready = sem("std_ready")
        ms_turned = sem("ms_turned")
        msT_copied = sem("msT_copied")
        mx_ready = sem("mx_ready")
        post_done = sem("post_done")
        za_ready = sem("za_ready")
        plain_ready = sem("plain_ready")
        z_ready = sem("z_ready")
        st2_ready = sem("st2_ready")
        mv2_ready = sem("mv2_ready")
        sd2_ready = sem("sd2_ready")
        rs2_ready = sem("rs2_ready")
        zo_ready = sem("zo_ready")
        worst_ready = sem("worst_ready")
        over_ready = sem("over_ready")
        over_summed = sem("over_summed")
        flag_ready = sem("flag_ready")
        rounds_set = sem("rounds_set")
        carry_ready = sem("carry_ready")
        w_loaded = sem("w_loaded")
        adj_loaded = [sem("adj_loaded0"), sem("adj_loaded1")]
        x_loaded = [sem("x_loaded0"), sem("x_loaded1")]
        out_stored = [sem("out_stored0"), sem("out_stored1")]
        gcn_w_loaded = sem("gcn_w_loaded")
        N_W = 9
        N_GCN_W = 8
        N_CONST = 12
        poolstep = sem("poolstep")

        def past(count):
            return max(count, 0) if isinstance(count, int) else count

        def every_turn(eng, gcn, means, post, before, turn, flag_step=None):
            def graph(b):
                return b, b % 2, b // 2

            gcn(*graph(0))
            means(*graph(0))
            before(*graph(0))
            gcn(*graph(1))
            turn(graph(2), graph(1), graph(0), None)
            for b in (1, 2):
                turn(graph(b + 2), graph(b + 1), graph(b), graph(b - 1))
            with eng.Fori(1, B // 2 - 2) as i:
                turn((2 * i + 3, 1, i + 1), (2 * i + 2, 0, i + 1), (2 * i + 1, 1, i), (2 * i, 0, i))
                turn((2 * i + 4, 0, i + 2), (2 * i + 3, 1, i + 1), (2 * i + 2, 0, i + 1), (2 * i + 1, 1, i))
            turn(graph(B - 1), graph(B - 2), graph(B - 3), graph(B - 4))
            turn(None, graph(B - 1), graph(B - 2), graph(B - 3))
            if flag_step:
                flag_step()
            turn(None, None, graph(B - 1), graph(B - 2))
            post(*graph(B - 1))

        def tile_read(b, t):
            if t == 0:
                return best_started, past(b + 1)
            return best_updated, past((PAIRS - 1) * b + t)

        def over_flag(eng):
            eng.wait_ge(flag_ready, 1)
            return nc.values_load(flag[0:1, 0:1], engines=[eng.engine], min_val=0, max_val=P)

        def every_round(eng, one_round, at_end=None):
            with eng.If(over_flag(eng) > 0):
                with eng.Fori(0, B) as b:
                    with eng.Fori(0, ROUNDS // 2) as pair:
                        k = B // 2 + b * (ROUNDS // 2) + pair
                        for par in range(2):
                            one_round(2 * k + par, par, k, b, 2 * pair + par)
                if at_end:
                    at_end()

        block = ctx.enter_context(nc.Block())

        @block.sync
        def _(sp):
            def w(dst, src, loaded=w_loaded):
                sp.dma_start(dst, src).then_inc(loaded, 16)

            def load(b, par, k, graph=None):
                graph = b if graph is None else graph
                sp.wait_ge(adj_turned, past(b - 1))
                sp.dma_start(adjn[:, par, :, :], adj_v[:, bass.ds(2 * graph, 2), :]).then_inc(adj_loaded[par], 16)
                sp.wait_ge(y_ready, past(2 * (b - 1)))
                sp.dma_start(xa[:, par, :, 0:D], x_v[:, bass.ds(2 * graph, 2), :]).then_inc(x_loaded[par], 16)

            load(0, 0, 0)
            w(W0b[0:D, :], W0, gcn_w_loaded)
            w(W0b[D:D + 1, :], b0[None, :], gcn_w_loaded)
            w(W1s[:, :], W1, gcn_w_loaded)
            w(brow[D:D + 1, 0, :], b1[None, :], gcn_w_loaded)
            w(brow[D:D + 1, 1, :], b2[None, :], gcn_w_loaded)
            w(W2s[:, :], W2, gcn_w_loaded)
            w(Wouts[:, :], Wout, gcn_w_loaded)
            w(boutr[:, :], bout[None, :], gcn_w_loaded)
            load(1, 1, 0)
            w(maskrows[:, :], mask_v)
            w(Wuv[0:D, 0:2, :], W_pre.rearrange("(a k) d -> k a d", a=2))
            sp.wait_ge(rows_filled, 3)
            w(Wuv[D:D + 1, 0, :], b_pre[None, :])
            w(Wx[0:D, :], W_post[0:D, :])
            w(Wx[D:D + 1, :], b_post[None, :])
            W_post_v = W_post[D:, :].rearrange("(c f k) d -> f k c d", c=3, f=4)
            w(Wst[0:D, :, :], W_post_v[0])
            w(Wst[D:P, :, :], W_post_v[3])
            w(Wmx[0:D, :, :], W_post_v[1])
            w(Wmx[D:P, :, :], W_post_v[2])
            with sp.Fori(0, B // 2 - 1) as i:
                load(2 * i + 2, 0, i + 1)
                load(2 * i + 3, 1, i + 1)

            def all_stored(graphs):
                for par in range(2):
                    sp.wait_ge(out_stored[par], 16 * (graphs // 2))

            all_stored(B)
            every_round(sp, lambda v, par, k, graph, r: load(v, par, k, graph),
                        lambda: all_stored(B + B * ROUNDS))

        @block.tensor
        def _(pe):
            mm = nc.tensor.matmul

            pe.wait_ge(consts_set, N_CONST)

            def constants():
                pe.wait_ge(w_loaded, 16 * N_W)
                nc.tensor.transpose(pC[0:P, 0:NH * B], maskrows[:, :], ident[0:NH * B, 0:NH * B])\
                    .then_inc(mask_turned, 1)
                pe.wait_ge(wsq_ready, 1)
                mm(pU[:, 0:D], ones64[:, :], Wsq[:, :], start=True, stop=True).then_inc(wsq_summed, 1)

            def turn_adj(b, par, k):
                pe.wait_ge(adj_loaded[par], 16 * (k + 1))
                pe.wait_ge(adjT_copied, past(b))
                pe.wait_ge(total_ready, past(b))
                pe.wait_ge(most_ready, past(b))
                for mh in range(NH):
                    for nh in range(NH):
                        o = (mh * NH + nh) * P
                        ins = nc.tensor.transpose(pT[:, o:o + P], adjn[:, par, nh, mh * P:(mh + 1) * P], ident[:, :])
                ins.then_inc(adj_turned, 1)

            def agg0(b, par, k):
                pe.wait_ge(x_loaded[par], 16 * (k + 1))
                pe.wait_ge(adjT_copied, b + 1)
                pe.wait_ge(y_ready, past(2 * b))
                for mh in range(NH):
                    ins = mm(pG[0:D + 1, 0:N], xa[:, par, mh, :], adjT[:, par, mh, :], start=(mh == 0), stop=(mh == 1))
                ins.then_inc(agg0_done, 1)

            def h1(b):
                pe.wait_ge(aggT_copied, b + 1)
                mm(pG[:, 0:N], W0b[:, :], aggT[:, :], start=True, stop=True).then_inc(h1_done, 1)

            def msg_mm(b, h_relu, W, done):
                pe.wait_ge(h_relu, b + 1)
                for nh in range(NH):
                    ins = mm(pG[:, nh * H:(nh + 1) * H], hT[:, nh * P:(nh + 1) * P], W[:, :], start=True, stop=True)
                ins.then_inc(done, 1)

            def agg_mm(b, par, msg_ready, layer, done):
                pe.wait_ge(msg_ready, b + 1)
                mm(pG[:, 0:N], brow[D:D + 1, layer, :], aggT[D:D + 1, :], start=True, stop=False)
                for mh in range(NH):
                    ins = mm(pG[:, 0:N], msg[:, mh, :], adjT[:, par, mh, :], start=False, stop=(mh == 1))
                ins.then_inc(done, 1)

            def count(b, par):
                pe.wait_ge(maskT_ready, b + 1)
                for nh in range(NH):
                    for mh in range(NH):
                        o = nh * NH + mh
                        ins = mm(pT[:, o:o + 1], maskT[:, par, mh, nh * P:(nh + 1) * P], ones[:, :], start=True, stop=True)
                ins.then_inc(counts_done, 1)

            def number(b, par):
                pe.wait_ge(maskT_ready, b + 1)
                pe.wait_ge(z_ready, past(2 * (b - 1)))
                for h in range(NH):
                    ins = mm(pC[:, h * N:(h + 1) * N], tri[:, :], maskT[:, par, h, :], start=True, stop=True)
                ins.then_inc(nums_done, 1)

            def out_mm(b):
                pe.wait_ge(h3_relu, b + 1)
                for nh in range(NH):
                    dst = pG[:, nh * D:(nh + 1) * D]
                    mm(dst, onerow[:, :], boutr[:, :], start=True, stop=False)
                    ins = mm(dst, hT[:, nh * P:(nh + 1) * P], Wouts[:, :], start=False, stop=True)
                ins.then_inc(yout_done, 1)

            def turn_x1(b, par):
                pe.wait_ge(x1_ready, 2 * b + 2)
                pe.wait_ge(iso_ready, b + 1)
                pe.wait_ge(q_ready, past(2 * b))
                pe.wait_ge(deg_copied, past(b))
                for nh in range(NH):
                    ins = nc.tensor.transpose(pU[:, nh * P:(nh + 1) * P], x1[:, par, nh, :], ident[:, :])
                ins.then_inc(x1_turned, 1)

            def uv(b, par):
                pe.wait_ge(x1T_copied, b + 1)
                for nh in range(NH):
                    ins = mm(pU_uv[:, nh, :], x1T[:, par, nh * P:(nh + 1) * P], Wuv[:, :, :].rearrange("k a b -> k (a b)"),
                             start=True, stop=True)
                ins.then_inc(uv_done, 1)

            def slots(b, par, t):
                pe.wait_ge(onehot_ready, 2 * PAIRS * b + 2 * t + 2)
                if t == 0:
                    pe.wait_ge(vhi_ready, b + 1)
                    pe.wait_ge(vlo_ready, b + 1)
                read, count = tile_read(b, t - 2) if t >= 2 else tile_read(b - 1, PAIRS + t - 2)
                pe.wait_ge(read, count)
                dst = pS[(par * PAIRS + t) % 2]
                for h in range(NH):
                    o = dst[:, h * 512:(h + 1) * 512]
                    oh = onehot[:, t, h, :, :].rearrange("p j n -> p (j n)")
                    mm(o, vhi[:, par, h, :], oh, start=True, stop=False)
                    ins = mm(o, vlo[:, par, h, :], oh.bitcast(bf16), start=False, stop=True)
                ins.then_inc(slot_done, 1)

            def sums(b, par):
                pe.wait_ge(v_copied, b + 1)
                pe.wait_ge(vsq_ready, b + 1)
                pe.wait_ge(u_copied, b + 1)
                pe.wait_ge(vhi_ready, b + 1)
                pe.wait_ge(vres_ready, b + 1)
                for nh in range(NH):
                    for mh in range(NH):
                        ins = mm(pU_s[:, nh, :], adjT[:, par, mh, nh * P:(nh + 1) * P], vv[:, mh, :],
                                 start=(mh == 0), stop=(mh == 1))
                ins.then_inc(sums_done, 1)

            def turn_ms(b, par, coded=None):
                pe.wait_ge(mean_ready, 2 * b + 2)
                pe.wait_ge(std_ready, b + 1)
                pe.wait_ge(code_ready, (min(b + 2, B) if isinstance(b, int) else b + 2) if coded is None else coded)
                pe.wait_ge(z_ready, past(2 * b))
                for nh in range(NH):
                    nc.tensor.transpose(pC[:, nh * P:(nh + 1) * P], ms[:, par, nh, :], ident[:, :])
                mm(pC[:, N:2 * N], Wum[:, :, :].rearrange("k a b -> k (a b)"), x1T[:, par, :], start=True, stop=True)\
                    .then_inc(ms_turned, 1)

            def finish(b, par):
                pe.wait_ge(msT_copied, b + 1)
                pe.wait_ge(mx_ready, b + 1)
                for nh in range(NH):
                    n = slice(nh * P, (nh + 1) * P)
                    mm(pC_y[:, nh, :], msT[:, n], Wst[:, :, :].rearrange("k a b -> k (a b)"), start=True, stop=False)
                    mm(pC_y[:, nh, 0:D], x1T[:, par, n], Wx[:, :], start=False, stop=False, skip_group_check=True)
                    ins = mm(pC_y[:, nh, :], mx[:, n], Wmx[:, :, :].rearrange("k a b -> k (a b)"), start=False, stop=True)
                ins.then_inc(post_done, 1)

            def gcn(b, par, k):
                turn_adj(b, par, k)
                if isinstance(b, int) and b == 0:
                    pe.wait_ge(gcn_w_loaded, 16 * N_GCN_W)
                agg0(b, par, k)
                h1(b)
                count(b, par)
                msg_mm(b, h1_relu, W1s, msg1_done)
                agg_mm(b, par, msg1_ready, 0, h2_done)
                msg_mm(b, h2_relu, W2s, msg2_done)
                agg_mm(b, par, msg2_ready, 1, h3_done)
                out_mm(b)
                if isinstance(b, int) and b == 0:
                    constants()

            def means(b, par, k):
                if isinstance(b, int) and b == 0:
                    pe.wait_ge(nmask_ready, 1)
                turn_x1(b, par)
                number(b, par)
                if isinstance(b, int) and b == 0:
                    pe.wait_ge(wcopies_ready, 4)
                    pe.wait_ge(wrows_ready, 4)
                    pe.wait_ge(wpost_neg, 1)
                    pe.wait_ge(wx_ready, 1)
                uv(b, par)
                sums(b, par)

            def post(b, par, k):
                turn_ms(b, par)
                finish(b, par)

            def before(b, par, k):
                pass

            def turn(ga, gn, gb, gc):
                b, bpar, _ = gb
                slots(b, bpar, 0)
                if ga:
                    turn_adj(*ga)
                if gc:
                    turn_ms(*gc[:2])
                slots(b, bpar, 1)
                if ga:
                    agg0(*ga)
                if gn:
                    turn_x1(*gn[:2])
                slots(b, bpar, 2)
                if ga:
                    h1(ga[0])
                    count(*ga[:2])
                if gc:
                    finish(*gc[:2])
                if ga:
                    msg_mm(ga[0], h1_relu, W1s, msg1_done)
                slots(b, bpar, 3)
                if gn:
                    uv(*gn[:2])
                if ga:
                    agg_mm(ga[0], ga[1], msg1_ready, 0, h2_done)
                slots(b, bpar, 4)
                if gn:
                    number(*gn[:2])
                if ga:
                    msg_mm(ga[0], h2_relu, W2s, msg2_done)
                if gn:
                    sums(*gn[:2])
                slots(b, bpar, 5)
                if ga:
                    agg_mm(ga[0], ga[1], msg2_ready, 1, h3_done)
                slots(b, bpar, 6)
                if ga:
                    out_mm(ga[0])

            def sum_over():
                pe.wait_ge(over_ready, 1)
                mm(pT[0:1, 0:1], ones[:, :], over[:, :], start=True, stop=True).then_inc(over_summed, 1)

            def one_round(v, par, k, graph, r):
                gcn(v, par, k)
                means(v, par, k)
                for t in range(PAIRS):
                    slots(v, par, t)
                turn_ms(v, par, coded=v + 1)
                finish(v, par)

            every_turn(pe, gcn, means, post, before, turn, sum_over)
            every_round(pe, one_round)

        @block.scalar
        def _(act):
            af = nc.scalar.activation
            act.wait_ge(consts_set, N_CONST)

            def constants():
                act.wait_ge(wsq_summed, 1)
                af(shift0[:, :], pU[:, 0:D], ACT.Sqrt, scale=XNORM * XNORM).then_inc(shift0_ready, 1)

            def copy_adjT(b, par):
                act.wait_ge(adj_turned, b + 1)
                act.wait_ge(sums_done, past(b - 1))
                af(adjT[:, par, :, :].rearrange("p h n -> p (h n)"), pT[:, :], ACT.Copy).then_inc(adjT_copied, 1)

            def copy_agg0(b):
                act.wait_ge(agg0_done, b + 1)
                af(aggT[:, :], pG[0:D + 1, 0:N], ACT.Copy).then_inc(aggT_copied, 1)

            def relu(b, src, dst):
                act.wait_ge(src, b + 1)
                af(hT[:, :], pG[:, 0:N], ACT.Relu).then_inc(dst, 1)

            def copy_code(b, par, r=None):
                act.wait_ge(nums_done, b + 1)
                act.wait_ge(onehot_ready, past(2 * PAIRS * (b - 1)))
                dst = code[:, par, :, :].rearrange("p h n -> p (h n)")
                if r is None:
                    af(dst, pC[:, :], ACT.Copy).then_inc(code_ready, 1)
                else:
                    af(dst, pC[:, :], ACT.Identity, bias=back[:, bass.ds(r, 1)]).then_inc(code_ready, 1)

            def copy_msg(b, src, dst):
                act.wait_ge(src, b + 1)
                af(msg[:, :, :].rearrange("p h c -> p (h c)"), pG[:, 0:N], ACT.Copy).then_inc(dst, 1)

            def sd_1(b):
                act.wait_ge(mv1_ready, 2 * b + 2)
                af(sd1[:, :], mv1[:, :, 1], ACT.Sqrt, bias=epscol[:, 0:1]).then_inc(sd1_ready, 1)

            def copy_x1T(b, par):
                act.wait_ge(x1_turned, b + 1)
                act.wait_ge(post_done, past(b - 1))
                af(x1T[:, par, :], pU[0:D + 2, 0:N], ACT.Copy).then_inc(x1T_copied, 1)

            def v_parts(b, par):
                act.wait_ge(uv_done, b + 1)
                act.wait_ge(slot_done, past(PAIRS * (b - 1)))
                af(vhi[:, par, :, :], pU_uv[:, :, 2 * D:4 * D], ACT.Copy).then_inc(vhi_ready, 1)
                act.wait_ge(uc_ready, past(b))
                act.wait_ge(mean_ready, past(2 * b))
                af(us[:, :, :], pU_uv[:, :, 0:D], ACT.Copy).then_inc(u_copied, 1)
                act.wait_ge(sums_done, past(b))
                af(vv[:, :, 0:D], pU_uv[:, :, D:2 * D], ACT.Copy).then_inc(v_copied, 1)
                af(vv[:, :, D:2 * D], pU_uv[:, :, D:2 * D], ACT.Square).then_inc(vsq_ready, 1)

            def start_best(b, par):
                act.wait_ge(slot_done, PAIRS * b + 1)
                act.wait_ge(best2_ready, past(b))
                af(best[:, :, :, :].rearrange("p h j n -> p (h j n)"), pS[(par * PAIRS) % 2][:, :], ACT.Copy)\
                    .then_inc(best_started, 1)

            def log_deg(b):
                act.wait_ge(deg_copied, b + 1)
                act.wait_ge(lgs_ready, past(b))
                act.wait_ge(amp_ready, past(b))
                af(lg[:, :], deg[:, :], ACT.Ln, bias=1.0).then_inc(lg_ready, 1)

            def std(b, par):
                act.wait_ge(var1_ready, b + 1)
                act.wait_ge(ms_turned, past(b - 1))
                af(ms[:, par, :, D:2 * D], var1[:, :, :], ACT.Sqrt).then_inc(std_ready, 1)

            def copy_msT(b):
                act.wait_ge(ms_turned, b + 1)
                act.wait_ge(post_done, past(b))
                act.wait_ge(mx_ready, b + 1)
                af(msT[:, :], pC[:, 0:N], ACT.Copy).then_inc(msT_copied, 1)

            def copy_plain(b):
                act.wait_ge(post_done, b + 1)
                act.wait_ge(za_ready, past(2 * b))
                af(plain[:, :, :], pC_y[:, :, 0:D], ACT.Copy).then_inc(plain_ready, 1)

            def sd_2(b):
                act.wait_ge(mv2_ready, 2 * b + 2)
                af(sd2[:, :], mv2[:, :, 1], ACT.Sqrt, bias=epscol[:, 0:1]).then_inc(sd2_ready, 1)

            def store(b, par, k, graph=None):
                graph = b if graph is None else graph
                act.wait_ge(zo_ready, 2 * b + 2)
                act.dma_start(out_v[:, bass.ds(2 * graph, 2), :], zo[:, par, :, :]).then_inc(out_stored[par], 16)

            def gcn(b, par, k):
                copy_adjT(b, par)
                copy_agg0(b)
                relu(b, h1_done, h1_relu)
                copy_msg(b, msg1_done, msg1_ready)
                relu(b, h2_done, h2_relu)
                copy_msg(b, msg2_done, msg2_ready)
                relu(b, h3_done, h3_relu)
                if isinstance(b, int) and b == 0:
                    constants()

            def means(b, par, k, r=None):
                sd_1(b)
                copy_x1T(b, par)
                copy_code(b, par, r)
                v_parts(b, par)
                log_deg(b)
                std(b, par)

            def slots(b, par):
                start_best(b, par)

            def post(b, par, k):
                copy_msT(b)
                copy_plain(b)
                sd_2(b)
                store(b, par, k)

            def before(b, par, k):
                pass

            def turn(ga, gn, gb, gc):
                b, bpar, _ = gb
                start_best(b, bpar)
                if gn:
                    sd_1(gn[0])
                if ga:
                    copy_adjT(*ga[:2])
                if gc:
                    copy_msT(gc[0])
                if ga:
                    copy_agg0(ga[0])
                if gn:
                    copy_x1T(*gn[:2])
                if ga:
                    relu(ga[0], h1_done, h1_relu)
                if gc:
                    copy_plain(gc[0])
                if ga:
                    copy_msg(ga[0], msg1_done, msg1_ready)
                if gc:
                    sd_2(gc[0])
                    store(*gc)
                if gn:
                    v_parts(*gn[:2])
                if ga:
                    relu(ga[0], h2_done, h2_relu)
                if gn:
                    copy_code(*gn[:2])
                if ga:
                    copy_msg(ga[0], msg2_done, msg2_ready)
                if gn:
                    log_deg(gn[0])
                if ga:
                    relu(ga[0], h3_done, h3_relu)
                if gn:
                    std(*gn[:2])

            def one_round(v, par, k, graph, r):
                act.wait_ge(rounds_set, ROUNDS + 3)
                gcn(v, par, k)
                means(v, par, k, r)
                slots(v, par)
                copy_msT(v)
                copy_plain(v)
                sd_2(v)
                act.wait_ge(out_stored[1 - par], 16 * (k + par))
                store(v, par, k, graph)

            every_turn(act, gcn, means, post, before, turn)
            every_round(act, one_round)

        @block.vector
        def _(dve):
            v = nc.vector
            v.memset(xa[:, 0, :, D:D + 1], 1.0).then_inc(consts_set, 1)
            v.memset(xa[:, 1, :, D:D + 1], 1.0).then_inc(consts_set, 1)
            v.memset(onerow[:, :], 1.0).then_inc(consts_set, 1)
            v.memset(Wuv[D:D + 2, :, :], 0.0).then_inc(rows_filled, 1)
            v.memset(Wum[D:D + 2, :, :], -BIG).then_inc(rows_filled, 1)
            v.memset(Wx[D:D + 2, :], 0.0).then_inc(rows_filled, 1)
            v.memset(x1[:, :, :, :], 1.0).then_inc(consts_set, 1)
            v.memset(vv[:, :, 2 * D:2 * D + 1], 1.0).then_inc(consts_set, 1)
            v.memset(epscol[:, :], EPS).then_inc(consts_set, 1)
            v.memset(lo_scale[:, :], LO).then_inc(consts_set, 1)
            v.memset(most[:, :, :], 0.0).then_inc(consts_set, 1)
            v.memset(ones[:, :], 1.0).then_inc(consts_set, 1)
            v.memset(ones64[:, :], 1.0).then_inc(consts_set, 1)
            dve.wait_ge(consts_set, N_CONST)
            dve.wait_ge(rows_filled, 3)

            def constants():
                dve.wait_ge(w_loaded, 16 * N_W)
                v.tensor_tensor(Wsq[:, :], Wuv[0:D, 1, :], Wuv[0:D, 1, :], ALU.mult).then_inc(wsq_ready, 1)
                v.tensor_copy(Wuv[0:D, 2, :], Wuv[0:D, 1, :]).then_inc(wcopies_ready, 1)
                v.tensor_scalar(Wuv[0:D, 3, :], Wuv[0:D, 1, :], -1.0, None, ALU.mult).then_inc(wcopies_ready, 1)
                v.tensor_copy(Wum[0:D, 0, :], Wuv[0:D, 0, :]).then_inc(wcopies_ready, 1)
                v.tensor_scalar(Wum[0:D, 1, :], Wuv[0:D, 0, :], -1.0, None, ALU.mult).then_inc(wcopies_ready, 1)
                v.tensor_tensor(Wx[0:D, :], Wx[0:D, :], ident[0:D, 0:D], ALU.add).then_inc(wx_ready, 1)
                v.tensor_scalar(Wmx[D:P, :, :], Wmx[D:P, :, :], -1.0, None, ALU.mult).then_inc(wpost_neg, 1)
                dve.wait_ge(mask_turned, 1)
                v.tensor_copy(nmask[:, :], pC[:, 0:NH * B]).then_inc(nmask_ready, 1)
                dve.wait_ge(shift0_ready, 1)
                row = slice(D, D + 1)
                for i in range(2):
                    v.tensor_copy(Wuv[row, 2 + i, :], shift0[row, :]).then_inc(wrows_ready, 1)
                v.tensor_tensor(Wum[row, 0, :], Wuv[row, 0, :], shift0[row, :], ALU.subtract).then_inc(wrows_ready, 1)
                v.scalar_tensor_tensor(out=Wum[row, 1, :], in0=Wuv[row, 0, :], scalar=-1.0, in1=shift0[row, :],
                                       op0=ALU.mult, op1=ALU.subtract).then_inc(wrows_ready, 1)
                dve.wait_ge(nmask_ready, 1)

            def get_mask(b, par):
                dve.wait_ge(adjT_copied, b + 1)
                dve.wait_ge(nums_done, past(b - 1))
                dve.wait_ge(counts_done, past(b - 1))
                v.tensor_scalar(maskT[:, par, :, :].rearrange("p h n -> p (h n)"),
                                adjT[:, par, :, :].rearrange("p h n -> p (h n)"), 0.0, None, ALU.is_gt)\
                    .then_inc(maskT_ready, 1)

            def count(b, par):
                dve.wait_ge(counts_done, b + 1)
                v.tensor_reduce(total[:, :], pT[:, 0:NH * NH].rearrange("p (a b) -> p a b", a=NH), AX, ALU.add)\
                    .then_inc(total_ready, 1)
                dve.wait_ge(most_ready, past(b))
                v.tensor_tensor(most[:, :, :], pT[:, 0:NH * NH].rearrange("p (a b) -> p a b", a=NH), most[:, :, :],
                                ALU.max).then_inc(most_ready, 1)
                dve.wait_ge(total_ready, b + 1)
                dve.wait_ge(x1_turned, past(b - 1))
                v.tensor_scalar(x1[:, par, :, D + 1], total[:, :], 0.0, None, ALU.is_equal).then_inc(iso_ready, 1)

            def residual(b, par, graph=None):
                graph = b if graph is None else graph
                dve.wait_ge(yout_done, b + 1)
                for h in range(NH):
                    v.scalar_tensor_tensor(out=y[:, h, :], in0=pG[:, h * D:(h + 1) * D],
                                           scalar=nmask[:, bass.ds(2 * graph + h, 1)],
                                           in1=xa[:, par, h, 0:D], op0=ALU.mult, op1=ALU.add).then_inc(y_ready, 1)

            def stats(b, src, ready, st, st_ready, mv, mv_ready):
                for h in range(NH):
                    dve.wait_ge(ready, 2 * b + 1 + h)
                    v.bn_stats(st[:, h, :], src[:, h, :]).then_inc(st_ready, 1)
                dve.wait_ge(st_ready, 2 * b + 2)
                v.memset(gate[:, :], 0.0)
                for h in range(NH):
                    v.bn_aggr(mv[:, h, :], st[:, h, :]).then_inc(mv_ready, 1)

            def norm(b, src, mv, sd, sd_ready, rs, rs_ready, dst, dst_ready):
                dve.wait_ge(sd_ready, b + 1)
                v.reciprocal(rs[:, :], sd[:, :]).then_inc(rs_ready, 1)
                dve.wait_ge(rs_ready, b + 1)
                for h in range(NH):
                    v.tensor_scalar(dst[:, h, :], src[:, h, :], mv[:, h, 0:1], rs[:, h:h + 1],
                                    ALU.subtract, ALU.mult).then_inc(dst_ready, 1)

            def norm1(b, par):
                dve.wait_ge(x1_turned, past(b - 1))
                norm(b, y, mv1, sd1, sd1_ready, rs1, rs1_ready, x1[:, par, :, 0:D], x1_ready)

            def make_onehot(b, par, t):
                dve.wait_ge(slot_done, past(PAIRS * (b - 1) + t + 1))
                dve.wait_ge(code_ready, b + 1)
                for j in range(2):
                    v.tensor_scalar(onehot[:, t, :, j, :], code[:, par, :, :], float(RANK0 + 2 * t + j + 1), HALF,
                                    ALU.is_equal, ALU.mult).then_inc(onehot_ready, 1)

            def low_part(b, par):
                dve.wait_ge(vhi_ready, b + 1)
                dve.wait_ge(vsq_ready, b + 1)
                dve.wait_ge(vlo_ready, past(b))
                v.tensor_tensor(vres[:, :, :], pU_uv[:, :, 2 * D:4 * D], vhi[:, par, :, :], ALU.subtract)\
                    .then_inc(vres_ready, 1)

            def update_best(b, par, t):
                dve.wait_ge(slot_done, PAIRS * b + t + 1)
                if t == 1:
                    dve.wait_ge(best_started, b + 1)
                else:
                    dve.wait_ge(best_updated, (PAIRS - 1) * b + t - 1)
                bv = best[:, :, :, :].rearrange("p h j n -> p (h j n)")
                v.tensor_tensor(bv, pS[(par * PAIRS + t) % 2][:, :], bv, ALU.max).then_inc(best_updated, 1)

            def degrees(b, par):
                dve.wait_ge(sums_done, b + 1)
                v.tensor_copy(deg[:, :], pU_s[:, :, 2 * D]).then_inc(deg_copied, 1)
                dve.wait_ge(deg_copied, b + 1)
                v.tensor_scalar(degs[:, :], deg[:, :], 1.0, None, ALU.max).then_inc(degs_ready, 1)
                dve.wait_ge(degs_ready, b + 1)
                v.reciprocal(rdeg[:, :], degs[:, :]).then_inc(rdeg_ready, 1)
                dve.wait_ge(rdeg_ready, b + 1)
                v.tensor_tensor(ratio[:, :], deg[:, :], rdeg[:, :], ALU.mult).then_inc(ratio_ready, 1)
                dve.wait_ge(uc_ready, past(b))
                dve.wait_ge(vb_ready, past(b))
                dve.wait_ge(cs_ready, past(b))
                for h in range(NH):
                    v.tensor_scalar(q[:, h, :], pU_s[:, h, 0:2 * D], rdeg[:, h:h + 1], None, ALU.mult)\
                        .then_inc(q_ready, 1)
                dve.wait_ge(ratio_ready, b + 1)
                v.tensor_scalar(slack[:, :], ratio[:, :], -1.0, 1.0, ALU.mult, ALU.add).then_inc(slack_ready, 1)
                dve.wait_ge(u_copied, b + 1)
                dve.wait_ge(ms_turned, past(b - 1))
                for h in range(NH):
                    dve.wait_ge(q_ready, 2 * b + 1 + h)
                    v.scalar_tensor_tensor(out=ms[:, par, h, 0:D], in0=us[:, h, :], scalar=ratio[:, h:h + 1],
                                           in1=q[:, h, 0:D], op0=ALU.mult, op1=ALU.add).then_inc(mean_ready, 1)

            def scalers(b, par):
                dve.wait_ge(lg_ready, b + 1)
                dve.wait_ge(z_ready, past(2 * (b - 1)))
                v.tensor_scalar(lgs[:, :], lg[:, :], EPS, None, ALU.max).then_inc(lgs_ready, 1)
                v.tensor_scalar(amp[:, par, :], lg[:, :], 1.0 / AVG_D_LOG, None, ALU.mult).then_inc(amp_ready, 1)
                dve.wait_ge(lgs_ready, b + 1)
                v.reciprocal(att0[:, :], lgs[:, :]).then_inc(att0_ready, 1)
                dve.wait_ge(att0_ready, b + 1)
                v.tensor_scalar(att[:, par, :], att0[:, :], AVG_D_LOG, None, ALU.mult).then_inc(att_ready, 1)

            def variance(b):
                dve.wait_ge(uc_ready, b + 1)
                dve.wait_ge(vb_ready, b + 1)
                dve.wait_ge(slack_ready, b + 1)
                for h in range(NH):
                    v.scalar_tensor_tensor(out=var0[:, h, :], in0=uc[:, h, :], scalar=slack[:, h:h + 1],
                                           in1=vb[:, h, :], op0=ALU.mult, op1=ALU.add).then_inc(var0_ready, 1)
                dve.wait_ge(var0_ready, 2 * b + 2)
                dve.wait_ge(std_ready, past(b))
                v.tensor_scalar(var1[:, :, :], var0[:, :, :], 0.0, EPS, ALU.max, ALU.add).then_inc(var1_ready, 1)

            def fold_best(b):
                dve.wait_ge(best_updated, (PAIRS - 1) * (b + 1))
                v.tensor_tensor(best2[:, :, :], best[:, 0, :, :], best[:, 1, :, :], ALU.max).then_inc(best2_ready, 1)
                dve.wait_ge(best2_ready, b + 1)
                dve.wait_ge(mx_ready, past(b))
                v.tensor_tensor(best1[:, :], best2[:, 0, :], best2[:, 1, :], ALU.max).then_inc(best1_ready, 1)

            def carry_best(v, r):
                dve.wait_ge(best1_ready, v + 1)
                dve.wait_ge(mx_ready, past(v))
                nc.vector.scalar_tensor_tensor(out=carry[:, :], in0=carry[:, :], scalar=keep[:, bass.ds(r, 1)],
                                               in1=best1[:, :], op0=ALU.mult, op1=ALU.max)\
                    .then_inc(carry_ready, 1)

            def add_u(b, top=best1):
                dve.wait_ge(ms_turned, b + 1)
                dve.wait_ge(best1_ready, b + 1)
                dve.wait_ge(post_done, past(b))
                v.scalar_tensor_tensor(out=mx[:, :], in0=top[:, :], scalar=1.0 / HALF, in1=pC[:, N:2 * N],
                                       op0=ALU.mult, op1=ALU.add).then_inc(mx_ready, 1)

            def combine(b, par):
                dve.wait_ge(plain_ready, b + 1)
                dve.wait_ge(amp_ready, b + 1)
                dve.wait_ge(att_ready, b + 1)
                for h in range(NH):
                    v.scalar_tensor_tensor(out=za[:, h, :], in0=pC_y[:, h, D:2 * D], scalar=amp[:, par, h:h + 1],
                                           in1=plain[:, h, :], op0=ALU.mult, op1=ALU.add).then_inc(za_ready, 1)
                for h in range(NH):
                    dve.wait_ge(za_ready, 2 * b + 1 + h)
                    v.scalar_tensor_tensor(out=z[:, h, :], in0=pC_y[:, h, 2 * D:3 * D], scalar=att[:, par, h:h + 1],
                                           in1=za[:, h, :], op0=ALU.mult, op1=ALU.add).then_inc(z_ready, 1)
                stats(b, z, z_ready, st2, st2_ready, mv2, mv2_ready)

            def norm2(b, par, k):
                dve.wait_ge(out_stored[par], past(16 * k))
                norm(b, z, mv2, sd2, sd2_ready, rs2, rs2_ready, zo[:, par, :, :], zo_ready)

            def stats1(b):
                stats(b, y, y_ready, st1, st1_ready, mv1, mv1_ready)

            def gcn(b, par, k, graph=None):
                get_mask(b, par)
                count(b, par)
                if isinstance(b, int) and b == 0:
                    constants()
                residual(b, par, graph)

            def means(b, par, k):
                stats1(b)
                norm1(b, par)
                low_part(b, par)
                degrees(b, par)
                scalers(b, par)
                variance(b)

            def before(b, par, k):
                for t in range(2):
                    make_onehot(b, par, t)

            def slots(b, par, k):
                for t in range(2, PAIRS):
                    make_onehot(b, par, t)
                for t in range(1, PAIRS):
                    update_best(b, par, t)
                fold_best(b)

            def post(b, par, k):
                add_u(b)
                combine(b, par)
                norm2(b, par, k)

            def turn(ga, gn, gb, gc):
                b, bpar, _ = gb
                if gn:
                    stats1(gn[0])
                make_onehot(b, bpar, 2)
                if ga:
                    get_mask(*ga[:2])
                if gn:
                    norm1(*gn[:2])
                if gc:
                    add_u(gc[0])
                update_best(b, bpar, 1)
                make_onehot(b, bpar, 3)
                if ga:
                    count(*ga[:2])
                update_best(b, bpar, 2)
                make_onehot(b, bpar, 4)
                if gc:
                    combine(*gc[:2])
                update_best(b, bpar, 3)
                if gc:
                    norm2(*gc)
                if gn:
                    low_part(*gn[:2])
                make_onehot(b, bpar, 5)
                update_best(b, bpar, 4)
                make_onehot(b, bpar, 6)
                if gn:
                    degrees(*gn[:2])
                update_best(b, bpar, 5)
                if gn:
                    scalers(*gn[:2])
                    make_onehot(gn[0], gn[1], 0)
                    make_onehot(gn[0], gn[1], 1)
                    variance(gn[0])
                update_best(b, bpar, 6)
                if ga:
                    residual(*ga[:2])
                fold_best(b)

            def make_flag():
                dve.wait_ge(most_ready, B)
                v.tensor_reduce(worst[:, :], most[:, :, :].rearrange("p a b -> p (a b)"), AX, ALU.max)\
                    .then_inc(worst_ready, 1)
                dve.wait_ge(worst_ready, 1)
                v.tensor_scalar(over[:, :], worst[:, :], float(SLOTS), None, ALU.is_gt)\
                    .then_inc(over_ready, 1)
                dve.wait_ge(over_summed, 1)
                v.tensor_copy(flag[0:1, 0:1], pT[0:1, 0:1]).then_inc(flag_ready, 1)

            def one_round(n, par, k, graph, r):
                gcn(n, par, k, graph)
                means(n, par, k)
                before(n, par, k)
                slots(n, par, k)
                carry_best(n, r)
                dve.wait_ge(carry_ready, n - B + 1)
                add_u(n, carry)
                combine(n, par)
                norm2(n, par, k)

            every_turn(dve, gcn, means, post, before, turn, make_flag)
            dve.wait_ge(flag_ready, 1)
            with dve.If(over_flag(dve) > 0):
                for r in range(ROUNDS):
                    v.memset(back[:, r:r + 1], float(-SLOTS * r)).then_inc(rounds_set, 1)
                v.memset(carry[:, :], 0.0).then_inc(rounds_set, 1)
                v.memset(keep[:, 0:1], 0.0).then_inc(rounds_set, 1)
                v.memset(keep[:, 1:ROUNDS], 1.0).then_inc(rounds_set, 1)
                dve.wait_ge(rounds_set, ROUNDS + 3)
            every_round(dve, one_round)

        @block.gpsimd
        def _(pool):
            g = nc.gpsimd
            cs_ = consts_set
            g.memset(ident[:, :], 0.0).then_inc(poolstep, 1)
            g.memset(tri[:, :], 1.0).then_inc(poolstep, 1)
            pool.wait_ge(poolstep, 2)
            g.affine_select(out=ident[:, :], in_=ident[:, :], compare_op=ALU.not_equal, fill=1.0, base=0,
                            pattern=[[-1, P]], channel_multiplier=1).then_inc(consts_set, 1)
            g.affine_select(out=tri[:, :], in_=tri[:, :], compare_op=ALU.is_ge, fill=0.0, base=0,
                            pattern=[[1, P]], channel_multiplier=-1).then_inc(poolstep, 1)
            pool.wait_ge(poolstep, 3)
            g.affine_select(out=tri[:, :], in_=tri[:, :], compare_op=ALU.not_equal, fill=float(RANK0 + 1), base=0,
                            pattern=[[-1, P]], channel_multiplier=1).then_inc(consts_set, 1)

            def low(b, par):
                pool.wait_ge(vres_ready, b + 1)
                pool.wait_ge(slot_done, past(PAIRS * (b - 1)))
                g.tensor_tensor(vlo[:, par, :, :], vres[:, :, :], lo_scale[:, None, :].to_broadcast([P, NH, 2 * D]),
                                ALU.mult).then_inc(vlo_ready, 1)

            def terms(b, par):
                pool.wait_ge(q_ready, 2 * b + 2)
                g.tensor_tensor(q1sq[:, :, :], q[:, :, 0:D], q[:, :, 0:D], ALU.mult).then_inc(q1sq_ready, 1)
                pool.wait_ge(mean_ready, 2 * b + 2)
                g.tensor_tensor(cs[:, :, :], ms[:, par, :, 0:D], q[:, :, 0:D], ALU.add).then_inc(cs_ready, 1)
                pool.wait_ge(q1sq_ready, b + 1)
                pool.wait_ge(var0_ready, past(2 * b))
                g.tensor_tensor(vb[:, :, :], q[:, :, D:2 * D], q1sq[:, :, :], ALU.subtract).then_inc(vb_ready, 1)
                pool.wait_ge(cs_ready, b + 1)
                g.tensor_tensor(uc[:, :, :], us[:, :, :], cs[:, :, :], ALU.mult).then_inc(uc_ready, 1)

            def gcn(b, par, k):
                pass

            def means(b, par, k):
                low(b, par)
                terms(b, par)

            def before(b, par, k):
                pass

            def post(b, par, k):
                pass

            def turn(ga, gn, gb, gc):
                if gn:
                    means(*gn)

            def one_round(v, par, k, graph, r):
                low(v, par)
                terms(v, par)

            every_turn(pool, gcn, means, post, before, turn)
            every_round(pool, one_round)


_INS = ['x', 'adj', 'nodemask', 'L0_gnn_W0', 'L0_gnn_b0', 'L0_gnn_W1', 'L0_gnn_b1', 'L0_gnn_W2', 'L0_gnn_b2',
        'L0_gnn_Wout', 'L0_gnn_bout', 'L1_gnn_W_pre', 'L1_gnn_b_pre', 'L1_gnn_W_post', 'L1_gnn_b_post']


def kernel(**inputs):
    import numpy as _np
    import concourse.bacc as _bacc
    from concourse import mybir as _mybir
    from concourse.bass_utils import run_bass_kernel_spmd as _run

    nc = _bacc.Bacc("TRN2", target_bir_lowering=False, num_devices=1)
    arrays, args = {}, []
    for name in _INS:
        a = _np.ascontiguousarray(inputs[name])
        arrays[f"in_{name}_dram"] = a
        args.append(nc.dram_tensor(f"in_{name}_dram", a.shape, _mybir.dt.from_np(a.dtype), kind="ExternalInput").ap())
    shape = _np.asarray(inputs["x"]).shape
    args.append(nc.dram_tensor("out_dram", shape, _mybir.dt.float32, kind="ExternalOutput").ap())
    gcn_pna_program(nc, *args)
    r = _run(nc, [arrays], core_ids=[0])
    return r.results[0]["out_dram"]
```

```python
import concourse.bass as bass
from concourse import mybir
from contextlib import ExitStack


def gcn_pna_program(nc, x, adj, nodemask, W0, b0, W1, b1, W2, b2, Wout, bout,
                    W_pre, b_pre, W_post, b_post, out):
    f32, f16, bf16, i32 = mybir.dt.float32, mybir.dt.float16, mybir.dt.bfloat16, mybir.dt.int32
    ALU = mybir.AluOpType
    ACT = mybir.ActivationFunctionType
    AX = mybir.AxisListType.X

    B, N, D = x.shape
    H = W0.shape[1]
    P = 128
    NH = N // P
    PAIRS = 7
    SLOTS = 2 * PAIRS
    ROUNDS = -(-P // (2 * SLOTS)) * 2
    RANK0 = 1024
    HALF = 0.5
    LO = 2.0 ** 14
    BIG = 1e9
    XNORM = 8.01
    AVG_D_LOG = 4.86
    EPS = 1e-5
    assert NH == 2 and D == 64 and H == P

    adj_v = adj.rearrange("b (h p) m -> p (b h) m", p=P)
    x_v = x.rearrange("b (h p) d -> p (b h) d", p=P)
    out_v = out.rearrange("b (h p) d -> p (b h) d", p=P)
    mask_v = nodemask.rearrange("b (h p) -> (b h) p", p=P)

    ctx = ExitStack()
    with ctx:
        def sb(name, shape, dt=f32):
            return ctx.enter_context(nc.sbuf_tensor(name, shape, dt))

        def pb(name, shape):
            return ctx.enter_context(nc.psum_tensor(name, shape, f32))

        def sem(name):
            return ctx.enter_context(nc.semaphore(name))

        ident = sb("ident", [P, P])
        W0b = sb("W0b", [D + 1, H])
        W1s, W2s = sb("W1s", [H, H]), sb("W2s", [H, H])
        Wouts = sb("Wouts", [H, D])
        boutr = sb("boutr", [1, D])
        onerow = sb("onerow", [1, P])
        Wuv = sb("Wuv", [D + 2, 3, D])
        Wum = sb("Wum", [D + 2, 2, D])
        Wst = sb("Wst", [P, 3, D])
        Wmx = sb("Wmx", [P, 3, D])
        tri = sb("tri", [P, P], f16)
        ones = sb("ones", [P, 1], f16)
        ones64 = sb("ones64", [D, P])
        Wsq = sb("Wsq", [D, D])
        shift = sb("shift", [P, D])
        bias = sb("bias", [P, 2, H])
        epscol = sb("epscol", [P, 1])
        gate = sb("gate", [1, 1])
        lo_scale = sb("lo_scale", [P, 2 * D])
        maskrows = sb("maskrows", [NH * B, P])
        nmask = sb("nmask", [P, NH * B])

        adjn = sb("adjn", [P, 2, NH, N])
        adjT = sb("adjT", [P, 2, NH, N])
        maskT = sb("maskT", [P, 2, NH, N], f16)
        xa = sb("xa", [P, 2, NH, D + 1])
        aggT = sb("aggT", [D + 1, N])
        hT = sb("hT", [H, N])
        msg = sb("msg", [P, NH, H])
        gmask = sb("gmask", [P, NH])
        y0 = sb("y0", [P, NH, D])
        y = sb("y", [P, NH, D])

        st1 = sb("st1", [P, NH, 6])
        mv1 = sb("mv1", [P, NH, 2])
        sd1 = sb("sd1", [P, NH])
        rs1 = sb("rs1", [P, NH])
        nb1 = sb("nb1", [P, NH])
        x1 = sb("x1", [P, 2, NH, P])
        x1T = sb("x1T", [D + 2, 2, N])
        code = sb("code", [P, 2, NH, N], f16)
        most = sb("most", [P, NH, NH])
        total = sb("total", [P, NH])

        vhi = sb("vhi", [P, 2, NH, 2 * D], f16)
        vfull = sb("vfull", [P, NH, 2 * D])
        vres = sb("vres", [P, NH, 2 * D])
        vlo = sb("vlo", [P, 2, NH, 2 * D], f16)
        us = sb("us", [P, NH, D])
        xw = sb("xw", [P, 2, NH, D])
        vv = sb("vv", [P, NH, 2 * D + 1])

        onehot = sb("onehot", [P, PAIRS, NH, 2, N], f16)
        best = sb("best", [P, NH, 2, N])
        best2 = sb("best2", [P, 2, N])
        best1 = sb("best1", [P, N])

        deg = sb("deg", [P, 2, NH])
        degs = sb("degs", [P, NH])
        rdeg = sb("rdeg", [P, NH])
        ratio = sb("ratio", [P, NH])
        slack = sb("slack", [P, NH])
        lg = sb("lg", [P, 2, NH])
        lgs = sb("lgs", [P, 2, NH])
        amp = sb("amp", [P, 2, NH])
        att = sb("att", [P, 2, NH])
        att0 = sb("att0", [P, 2, NH])
        q = sb("q", [P, NH, 2 * D])
        ms = sb("ms", [P, 2, NH, 2 * D])
        q1sq = sb("q1sq", [P, NH, D])
        ru = sb("ru", [P, NH, D])
        su = sb("su", [P, NH, D])
        vb = sb("vb", [P, NH, D])
        cs = sb("cs", [P, NH, D])
        uc = sb("uc", [P, NH, D])
        var0 = sb("var0", [P, NH, D])
        var1 = sb("var1", [P, NH, D])
        msT = sb("msT", [P, N])
        mx = sb("mx", [P, N])
        scaled = sb("scaled", [P, 3, NH, D])
        za = sb("za", [P, NH, D])
        zb = sb("zb", [P, NH, D])
        z = sb("z", [P, NH, D])
        st2 = sb("st2", [P, NH, 6])
        mv2 = sb("mv2", [P, NH, 2])
        sd2 = sb("sd2", [P, NH])
        rs2 = sb("rs2", [P, NH])
        nb2 = sb("nb2", [P, NH])
        zo = sb("zo", [P, 2, NH, D])

        worst = sb("worst", [P, 1])
        over = sb("over", [P, 1], f16)
        flag = sb("flag", [1, 1], i32)
        back = sb("back", [P, ROUNDS])
        keep = sb("keep", [P, ROUNDS])
        carry = sb("carry", [P, N])

        pT = pb("pT", [P, 512])
        pG = pb("pG", [P, 512])
        pC = pb("pC", [P, 512])
        pU = pb("pU", [P, 512])
        pS = [pb(f"pS{i}", [P, 1024]) for i in range(2)]
        pU_uv = pU[:, 0:NH * 3 * D].rearrange("p (h c) -> p h c", h=NH)
        pU_s = pU[:, 0:NH * (2 * D + 1)].rearrange("p (h c) -> p h c", h=NH)
        pC_y = pC[:, 0:NH * 3 * D].rearrange("p (h c) -> p h c", h=NH)

        consts_set = sem("consts_set")
        mask_turned = sem("mask_turned")
        nmask_ready = sem("nmask_ready")
        wpost_neg = sem("wpost_neg")
        adj_turned = sem("adj_turned")
        adjT_copied = sem("adjT_copied")
        maskT_ready = sem("maskT_ready")
        agg0_done = sem("agg0_done")
        aggT_copied = sem("aggT_copied")
        nums_done = sem("nums_done")
        counts_done = sem("counts_done")
        h1_done = sem("h1_done")
        h1_relu = sem("h1_relu")
        msg1_done = sem("msg1_done")
        msg1_ready = sem("msg1_ready")
        h2_done = sem("h2_done")
        h2_relu = sem("h2_relu")
        msg2_done = sem("msg2_done")
        msg2_ready = sem("msg2_ready")
        h3_done = sem("h3_done")
        h3_relu = sem("h3_relu")
        wsq_ready = sem("wsq_ready")
        wsq_summed = sem("wsq_summed")
        shift_ready = sem("shift_ready")
        wrows_ready = sem("wrows_ready")
        wcopies_ready = sem("wcopies_ready")
        rows_filled = sem("rows_filled")
        yout_done = sem("yout_done")
        y_ready = sem("y_ready")
        st1_ready = sem("st1_ready")
        mv1_ready = sem("mv1_ready")
        sd1_ready = sem("sd1_ready")
        rs1_ready = sem("rs1_ready")
        x1_ready = sem("x1_ready")
        x1_turned = sem("x1_turned")
        x1T_copied = sem("x1T_copied")
        code_ready = sem("code_ready")
        total_ready = sem("total_ready")
        most_ready = sem("most_ready")
        iso_ready = sem("iso_ready")
        uv_done = sem("uv_done")
        vhi_ready = sem("vhi_ready")
        vfull_ready = sem("vfull_ready")
        vres_ready = sem("vres_ready")
        vlo_ready = sem("vlo_ready")
        u_copied = sem("u_copied")
        v_copied = sem("v_copied")
        vsq_ready = sem("vsq_ready")
        onehot_ready = sem("onehot_ready")
        slot_done = sem("slot_done")
        best_started = sem("best_started")
        best_updated = sem("best_updated")
        best2_ready = sem("best2_ready")
        wx_ready = sem("wx_ready")
        best1_ready = sem("best1_ready")
        sums_done = sem("sums_done")
        deg_copied = sem("deg_copied")
        lg_ready = sem("lg_ready")
        degs_ready = sem("degs_ready")
        rdeg_ready = sem("rdeg_ready")
        ratio_ready = sem("ratio_ready")
        slack_ready = sem("slack_ready")
        lgs_ready = sem("lgs_ready")
        amp_ready = sem("amp_ready")
        att0_ready = sem("att0_ready")
        att_ready = sem("att_ready")
        q_ready = sem("q_ready")
        mean_ready = sem("mean_ready")
        q1sq_ready = sem("q1sq_ready")
        vb_ready = sem("vb_ready")
        cs_ready = sem("cs_ready")
        uc_ready = sem("uc_ready")
        var0_ready = sem("var0_ready")
        var1_ready = sem("var1_ready")
        std_ready = sem("std_ready")
        ms_turned = sem("ms_turned")
        msT_copied = sem("msT_copied")
        mx_ready = sem("mx_ready")
        post_done = sem("post_done")
        za_ready = sem("za_ready")
        zb_ready = sem("zb_ready")
        xw_copied = sem("xw_copied")
        scaled_ready = sem("scaled_ready")
        y0_ready = sem("y0_ready")
        gmask_ready = sem("gmask_ready")
        nb1_ready = sem("nb1_ready")
        nb2_ready = sem("nb2_ready")
        ru_ready = sem("ru_ready")
        su_ready = sem("su_ready")
        z_ready = sem("z_ready")
        st2_ready = sem("st2_ready")
        mv2_ready = sem("mv2_ready")
        sd2_ready = sem("sd2_ready")
        rs2_ready = sem("rs2_ready")
        zo_ready = sem("zo_ready")
        worst_ready = sem("worst_ready")
        over_ready = sem("over_ready")
        over_summed = sem("over_summed")
        flag_ready = sem("flag_ready")
        rounds_set = sem("rounds_set")
        carry_ready = sem("carry_ready")
        w_loaded = sem("w_loaded")
        adj_loaded = [sem("adj_loaded0"), sem("adj_loaded1")]
        x_loaded = [sem("x_loaded0"), sem("x_loaded1")]
        out_stored = [sem("out_stored0"), sem("out_stored1")]
        gcn_w_loaded = sem("gcn_w_loaded")
        N_W = 9
        N_GCN_W = 8
        N_CONST = 12
        poolstep = sem("poolstep")

        def first(b):
            return isinstance(b, int) and b == 0

        def past(count):
            return max(count, 0) if isinstance(count, int) else count

        def every_turn(eng, gcn, post, turn, flag_step=None):
            def graph(b):
                return b, b % 2, b // 2

            gcn(*graph(0))
            turn(graph(1), graph(0), None, None)
            turn(graph(2), graph(1), graph(0), None)
            for b in (1, 2):
                turn(graph(b + 2), graph(b + 1), graph(b), graph(b - 1))
            with eng.Fori(1, B // 2 - 2) as i:
                turn((2 * i + 3, 1, i + 1), (2 * i + 2, 0, i + 1), (2 * i + 1, 1, i), (2 * i, 0, i))
                turn((2 * i + 4, 0, i + 2), (2 * i + 3, 1, i + 1), (2 * i + 2, 0, i + 1), (2 * i + 1, 1, i))
            turn(graph(B - 1), graph(B - 2), graph(B - 3), graph(B - 4))
            turn(None, graph(B - 1), graph(B - 2), graph(B - 3))
            if flag_step:
                flag_step()
            turn(None, None, graph(B - 1), graph(B - 2))
            post(*graph(B - 1))

        def tile_read(b, t):
            if t == 0:
                return best_started, past(b + 1)
            return best_updated, past((PAIRS - 1) * b + t)

        def over_flag(eng):
            eng.wait_ge(flag_ready, 1)
            return nc.values_load(flag[0:1, 0:1], engines=[eng.engine], min_val=0, max_val=P)

        def every_round(eng, one_round, at_end=None):
            with eng.If(over_flag(eng) > 0):
                with eng.Fori(0, B) as b:
                    with eng.Fori(0, ROUNDS // 2) as pair:
                        k = B // 2 + b * (ROUNDS // 2) + pair
                        for par in range(2):
                            one_round(2 * k + par, par, k, b, 2 * pair + par)
                if at_end:
                    at_end()

        block = ctx.enter_context(nc.Block())

        @block.sync
        def _(sp):
            def w(dst, src, loaded=w_loaded):
                sp.dma_start(dst, src).then_inc(loaded, 16)

            def load(b, par, k, graph=None):
                graph = b if graph is None else graph
                sp.wait_ge(adj_turned, past(b - 1))
                sp.dma_start(adjn[:, par, :, :], adj_v[:, bass.ds(2 * graph, 2), :]).then_inc(adj_loaded[par], 16)
                sp.wait_ge(y_ready, past(b - 1))
                sp.dma_start(xa[:, par, :, 0:D], x_v[:, bass.ds(2 * graph, 2), :]).then_inc(x_loaded[par], 16)

            load(0, 0, 0)
            w(W0b[0:D, :], W0, gcn_w_loaded)
            w(W0b[D:D + 1, :], b0[None, :], gcn_w_loaded)
            w(W1s[:, :], W1, gcn_w_loaded)
            w(bias[:, 0, :], b1[None, :].to_broadcast([P, H]), gcn_w_loaded)
            w(bias[:, 1, :], b2[None, :].to_broadcast([P, H]), gcn_w_loaded)
            w(W2s[:, :], W2, gcn_w_loaded)
            w(Wouts[:, :], Wout, gcn_w_loaded)
            w(boutr[:, :], bout[None, :], gcn_w_loaded)
            load(1, 1, 0)
            w(maskrows[:, :], mask_v)
            w(Wuv[0:D, 0:2, :], W_pre.rearrange("(a k) d -> k a d", a=2))
            sp.wait_ge(rows_filled, 2)
            w(Wuv[D:D + 1, 0, :], b_pre[None, :])
            w(Wuv[0:D, 2, :], W_post[0:D, :])
            w(Wuv[D:D + 1, 2, :], b_post[None, :])
            W_post_v = W_post[D:, :].rearrange("(c f k) d -> f k c d", c=3, f=4)
            w(Wst[0:D, :, :], W_post_v[0])
            w(Wst[D:P, :, :], W_post_v[3])
            w(Wmx[0:D, :, :], W_post_v[1])
            w(Wmx[D:P, :, :], W_post_v[2])
            with sp.Fori(0, B // 2 - 1) as i:
                load(2 * i + 2, 0, i + 1)
                load(2 * i + 3, 1, i + 1)

            def all_stored(graphs):
                for par in range(2):
                    sp.wait_ge(out_stored[par], 16 * (graphs // 2))

            all_stored(B)
            every_round(sp, lambda v, par, k, graph, r: load(v, par, k, graph),
                        lambda: all_stored(B + B * ROUNDS))

        @block.tensor
        def _(pe):
            mm = nc.tensor.matmul

            pe.wait_ge(consts_set, N_CONST)

            def constants():
                pe.wait_ge(w_loaded, 16 * N_W)
                nc.tensor.transpose(pC[0:P, 0:NH * B], maskrows[:, :], ident[0:NH * B, 0:NH * B])\
                    .then_inc(mask_turned, 1)
                pe.wait_ge(wsq_ready, 1)
                mm(pU[:, 0:D], ones64[:, :], Wsq[:, :], start=True, stop=True).then_inc(wsq_summed, 1)

            def turn_adj(b, par, k):
                pe.wait_ge(adj_loaded[par], 16 * (k + 1))
                pe.wait_ge(adjT_copied, past(b))
                pe.wait_ge(total_ready, past(b))
                pe.wait_ge(most_ready, past(b))
                for mh in range(NH):
                    for nh in range(NH):
                        o = (mh * NH + nh) * P
                        ins = nc.tensor.transpose(pT[:, o:o + P], adjn[:, par, nh, mh * P:(mh + 1) * P], ident[:, :])
                ins.then_inc(adj_turned, 1)

            def agg0(b, par, k):
                pe.wait_ge(x_loaded[par], 16 * (k + 1))
                pe.wait_ge(adjT_copied, b + 1)
                pe.wait_ge(y0_ready, past(2 * b))
                for mh in range(NH):
                    ins = mm(pG[0:D + 1, 0:N], xa[:, par, mh, :], adjT[:, par, mh, :], start=(mh == 0), stop=(mh == 1))
                ins.then_inc(agg0_done, 1)

            def h1(b):
                pe.wait_ge(aggT_copied, b + 1)
                mm(pG[:, 0:N], W0b[:, :], aggT[:, :], start=True, stop=True).then_inc(h1_done, 1)

            def msg_mm(b, h_relu, W, done):
                pe.wait_ge(h_relu, b + 1)
                for nh in range(NH):
                    ins = mm(pG[:, nh * H:(nh + 1) * H], hT[:, nh * P:(nh + 1) * P], W[:, :], start=True, stop=True)
                ins.then_inc(done, 1)

            def agg_mm(b, par, msg_ready, done):
                pe.wait_ge(msg_ready, b + 1)
                for mh in range(NH):
                    ins = mm(pG[:, 0:N], msg[:, mh, :], adjT[:, par, mh, :], start=(mh == 0), stop=(mh == 1))
                ins.then_inc(done, 1)

            def count(b, par):
                pe.wait_ge(maskT_ready, b + 1)
                for nh in range(NH):
                    for mh in range(NH):
                        o = nh * NH + mh
                        ins = mm(pT[:, o:o + 1], maskT[:, par, mh, nh * P:(nh + 1) * P], ones[:, :], start=True, stop=True)
                ins.then_inc(counts_done, 1)

            def number(b, par):
                if first(b):
                    pe.wait_ge(nmask_ready, 1)
                pe.wait_ge(maskT_ready, b + 1)
                pe.wait_ge(scaled_ready, past(5 * (b - 1)))
                for h in range(NH):
                    ins = mm(pC[:, h * N:(h + 1) * N], tri[:, :], maskT[:, par, h, :], start=True, stop=True)
                ins.then_inc(nums_done, 1)

            def out_mm(b):
                pe.wait_ge(h3_relu, b + 1)
                for nh in range(NH):
                    dst = pG[:, nh * D:(nh + 1) * D]
                    mm(dst, onerow[:, :], boutr[:, :], start=True, stop=False)
                    ins = mm(dst, hT[:, nh * P:(nh + 1) * P], Wouts[:, :], start=False, stop=True)
                ins.then_inc(yout_done, 1)

            def turn_x1(b, par):
                pe.wait_ge(x1_ready, 2 * b + 2)
                pe.wait_ge(iso_ready, b + 1)
                pe.wait_ge(q_ready, past(2 * b))
                pe.wait_ge(deg_copied, past(b))
                for nh in range(NH):
                    ins = nc.tensor.transpose(pU[:, nh * P:(nh + 1) * P], x1[:, par, nh, :], ident[:, :])
                ins.then_inc(x1_turned, 1)

            def uv(b, par):
                pe.wait_ge(x1T_copied, b + 1)
                if first(b):
                    pe.wait_ge(wcopies_ready, 2)
                    pe.wait_ge(wrows_ready, 2)
                    pe.wait_ge(wpost_neg, 1)
                    pe.wait_ge(wx_ready, 1)
                for nh in range(NH):
                    ins = mm(pU_uv[:, nh, :], x1T[:, par, nh * P:(nh + 1) * P], Wuv[:, :, :].rearrange("k a b -> k (a b)"),
                             start=True, stop=True)
                ins.then_inc(uv_done, 1)

            def slots(b, par, t):
                pe.wait_ge(onehot_ready, 2 * PAIRS * b + 2 * t + 2)
                if t == 0:
                    pe.wait_ge(vhi_ready, b + 1)
                    pe.wait_ge(vlo_ready, b + 1)
                read, count = tile_read(b, t - 2) if t >= 2 else tile_read(b - 1, PAIRS + t - 2)
                pe.wait_ge(read, count)
                dst = pS[(par * PAIRS + t) % 2]
                for h in range(NH):
                    o = dst[:, h * 512:(h + 1) * 512]
                    oh = onehot[:, t, h, :, :].rearrange("p j n -> p (j n)")
                    mm(o, vhi[:, par, h, :], oh, start=True, stop=False)
                    ins = mm(o, vlo[:, par, h, :], oh.bitcast(bf16), start=False, stop=True)
                ins.then_inc(slot_done, 1)

            def sum_neighbours(b, par):
                pe.wait_ge(v_copied, b + 1)
                pe.wait_ge(vsq_ready, b + 1)
                pe.wait_ge(u_copied, b + 1)
                pe.wait_ge(xw_copied, b + 1)
                for nh in range(NH):
                    for mh in range(NH):
                        ins = mm(pU_s[:, nh, :], adjT[:, par, mh, nh * P:(nh + 1) * P], vv[:, mh, :],
                                 start=(mh == 0), stop=(mh == 1))
                ins.then_inc(sums_done, 1)

            def turn_ms(b, par, coded=None):
                pe.wait_ge(mean_ready, b + 1)
                pe.wait_ge(std_ready, b + 1)
                pe.wait_ge(code_ready, (min(b + 2, B) if isinstance(b, int) else b + 2) if coded is None else coded)
                pe.wait_ge(scaled_ready, past(5 * b))
                for nh in range(NH):
                    nc.tensor.transpose(pC[:, nh * P:(nh + 1) * P], ms[:, par, nh, :], ident[:, :])
                mm(pC[:, N:2 * N], Wum[:, :, :].rearrange("k a b -> k (a b)"), x1T[:, par, :], start=True, stop=True)\
                    .then_inc(ms_turned, 1)

            def finish(b, par):
                pe.wait_ge(msT_copied, b + 1)
                pe.wait_ge(mx_ready, b + 1)
                for nh in range(NH):
                    n = slice(nh * P, (nh + 1) * P)
                    mm(pC_y[:, nh, :], msT[:, n], Wst[:, :, :].rearrange("k a b -> k (a b)"), start=True, stop=False)
                    ins = mm(pC_y[:, nh, :], mx[:, n], Wmx[:, :, :].rearrange("k a b -> k (a b)"), start=False, stop=True)
                ins.then_inc(post_done, 1)

            def gcn(b, par, k):
                turn_adj(b, par, k)
                if first(b):
                    pe.wait_ge(gcn_w_loaded, 16 * N_GCN_W)
                agg0(b, par, k)
                h1(b)
                count(b, par)
                msg_mm(b, h1_relu, W1s, msg1_done)
                agg_mm(b, par, msg1_ready, h2_done)
                msg_mm(b, h2_relu, W2s, msg2_done)
                agg_mm(b, par, msg2_ready, h3_done)
                if first(b):
                    constants()

            def sums(b, par, k):
                out_mm(b)
                turn_x1(b, par)
                number(b, par)
                uv(b, par)
                sum_neighbours(b, par)

            def post(b, par, k):
                turn_ms(b, par)
                finish(b, par)

            def turn(ga, gn, gb, gc):
                b, bpar, _ = gb or (None, None, None)
                if gc:
                    turn_ms(*gc[:2])
                if gn:
                    out_mm(gn[0])
                if gb:
                    slots(b, bpar, 0)
                if ga:
                    turn_adj(*ga)
                if gb:
                    slots(b, bpar, 1)
                    slots(b, bpar, 2)
                if ga:
                    agg0(*ga)
                if gc:
                    finish(*gc[:2])
                if gb:
                    slots(b, bpar, 3)
                if ga:
                    h1(ga[0])
                    count(*ga[:2])
                if gn:
                    turn_x1(*gn[:2])
                if gb:
                    slots(b, bpar, 4)
                if ga:
                    msg_mm(ga[0], h1_relu, W1s, msg1_done)
                if gn:
                    uv(*gn[:2])
                    number(*gn[:2])
                if gb:
                    slots(b, bpar, 5)
                if ga:
                    agg_mm(ga[0], ga[1], msg1_ready, h2_done)
                if gb:
                    slots(b, bpar, 6)
                if ga:
                    msg_mm(ga[0], h2_relu, W2s, msg2_done)
                if gn:
                    sum_neighbours(*gn[:2])
                if ga:
                    agg_mm(ga[0], ga[1], msg2_ready, h3_done)

            def sum_over():
                pe.wait_ge(over_ready, 1)
                mm(pT[0:1, 0:1], ones[:, :], over[:, :], start=True, stop=True).then_inc(over_summed, 1)

            def one_round(v, par, k, graph, r):
                gcn(v, par, k)
                sums(v, par, k)
                for t in range(PAIRS):
                    slots(v, par, t)
                turn_ms(v, par, coded=v + 1)
                finish(v, par)

            every_turn(pe, gcn, post, turn, sum_over)
            every_round(pe, one_round)

        @block.scalar
        def _(act):
            af = nc.scalar.activation
            act.wait_ge(consts_set, N_CONST)

            def constants():
                act.wait_ge(wsq_summed, 1)
                af(shift[:, :], pU[:, 0:D], ACT.Sqrt, scale=XNORM * XNORM).then_inc(shift_ready, 1)

            def copy_adjT(b, par):
                act.wait_ge(adj_turned, b + 1)
                act.wait_ge(sums_done, past(b - 1))
                af(adjT[:, par, :, :].rearrange("p h n -> p (h n)"), pT[:, :], ACT.Copy).then_inc(adjT_copied, 1)

            def copy_agg0(b):
                act.wait_ge(agg0_done, b + 1)
                af(aggT[:, :], pG[0:D + 1, 0:N], ACT.Copy).then_inc(aggT_copied, 1)

            def relu(b, src, dst):
                act.wait_ge(src, b + 1)
                af(hT[:, :], pG[:, 0:N], ACT.Relu).then_inc(dst, 1)

            def copy_code(b, par, r=None):
                act.wait_ge(nums_done, b + 1)
                act.wait_ge(onehot_ready, past(2 * PAIRS * (b - 1)))
                dst = code[:, par, :, :].rearrange("p h n -> p (h n)")
                if r is None:
                    af(dst, pC[:, :], ACT.Copy).then_inc(code_ready, 1)
                else:
                    af(dst, pC[:, :], ACT.Identity, bias=back[:, bass.ds(r, 1)]).then_inc(code_ready, 1)

            def scale_y(b):
                act.wait_ge(yout_done, b + 1)
                act.wait_ge(gmask_ready, b + 1)
                act.wait_ge(y_ready, past(b))
                for h in range(NH):
                    af(y0[:, h, :], pG[:, h * D:(h + 1) * D], ACT.Identity, scale=gmask[:, h:h + 1])\
                        .then_inc(y0_ready, 1)

            def sd_1(b):
                act.wait_ge(mv1_ready, 2 * b + 2)
                act.wait_ge(rs1_ready, past(b))
                af(sd1[:, :], mv1[:, :, 1], ACT.Sqrt, bias=epscol[:, 0:1]).then_inc(sd1_ready, 1)

            def norm1(b, par):
                act.wait_ge(nb1_ready, b + 1)
                act.wait_ge(x1_turned, past(b - 1))
                for h in range(NH):
                    af(x1[:, par, h, 0:D], y[:, h, :], ACT.Identity, bias=nb1[:, h:h + 1], scale=rs1[:, h:h + 1])\
                        .then_inc(x1_ready, 1)

            def copy_x1T(b, par):
                act.wait_ge(x1_turned, b + 1)
                act.wait_ge(ms_turned, past(b - 1))
                af(x1T[:, par, :], pU[0:D + 2, 0:N], ACT.Copy).then_inc(x1T_copied, 1)

            def v_parts(b, par):
                act.wait_ge(uv_done, b + 1)
                act.wait_ge(sums_done, past(b))
                act.wait_ge(vfull_ready, past(2 * b))
                af(vv[:, :, 0:D], pU_uv[:, :, D:2 * D], ACT.Copy).then_inc(v_copied, 1)
                af(vv[:, :, D:2 * D], pU_uv[:, :, D:2 * D], ACT.Square).then_inc(vsq_ready, 1)
                act.wait_ge(uc_ready, past(b))
                act.wait_ge(ru_ready, past(2 * b))
                af(us[:, :, :], pU_uv[:, :, 0:D], ACT.Copy).then_inc(u_copied, 1)
                act.wait_ge(zb_ready, past(b - 1))
                af(xw[:, par, :, :], pU_uv[:, :, 2 * D:3 * D], ACT.Copy).then_inc(xw_copied, 1)

            def high_part(b, par):
                act.wait_ge(vfull_ready, 2 * b + 2)
                act.wait_ge(slot_done, past(PAIRS * (b - 1)))
                af(vhi[:, par, :, :], vfull[:, :, :], ACT.Copy).then_inc(vhi_ready, 1)

            def start_best(b, par):
                act.wait_ge(slot_done, PAIRS * b + 1)
                act.wait_ge(best2_ready, past(b))
                af(best[:, :, :, :].rearrange("p h j n -> p (h j n)"), pS[(par * PAIRS) % 2][:, :], ACT.Copy)\
                    .then_inc(best_started, 1)

            def log_deg(b, graphs, which):
                act.wait_ge(deg_copied, b + 1)
                act.wait_ge(lgs_ready, past(b + 1 - graphs))
                act.wait_ge(amp_ready, past(b + 1 - graphs))
                af(lg[:, which, :], deg[:, which, :], ACT.Ln, bias=1.0).then_inc(lg_ready, graphs)

            def scale_q(b):
                act.wait_ge(rdeg_ready, b + 1)
                act.wait_ge(mean_ready, past(b))
                act.wait_ge(vb_ready, past(b))
                act.wait_ge(cs_ready, past(b))
                for h in range(NH):
                    af(q[:, h, :], pU_s[:, h, 0:2 * D], ACT.Identity, scale=rdeg[:, h:h + 1]).then_inc(q_ready, 1)

            def scale_u(b):
                act.wait_ge(ratio_ready, b + 1)
                act.wait_ge(u_copied, b + 1)
                act.wait_ge(mean_ready, past(b))
                for h in range(NH):
                    af(ru[:, h, :], us[:, h, :], ACT.Identity, scale=ratio[:, h:h + 1]).then_inc(ru_ready, 1)

            def scale_uc(b):
                act.wait_ge(slack_ready, b + 1)
                act.wait_ge(uc_ready, b + 1)
                act.wait_ge(var0_ready, past(b))
                for h in range(NH):
                    af(su[:, h, :], uc[:, h, :], ACT.Identity, scale=slack[:, h:h + 1]).then_inc(su_ready, 1)

            def std(b, par):
                act.wait_ge(var0_ready, b + 1)
                act.wait_ge(std_ready, past(b))
                af(var1[:, :, :], var0[:, :, :], ACT.Relu).then_inc(var1_ready, 1)
                act.wait_ge(var1_ready, b + 1)
                act.wait_ge(ms_turned, past(b - 1))
                af(ms[:, par, :, D:2 * D], var1[:, :, :], ACT.Sqrt, bias=epscol[:, 0:1]).then_inc(std_ready, 1)

            def copy_msT(b):
                act.wait_ge(ms_turned, b + 1)
                act.wait_ge(post_done, past(b))
                act.wait_ge(mx_ready, b + 1)
                af(msT[:, :], pC[:, 0:N], ACT.Copy).then_inc(msT_copied, 1)

            def scale_post(b, par):
                act.wait_ge(post_done, b + 1)
                act.wait_ge(amp_ready, b + 1)
                act.wait_ge(att_ready, b + 1)
                act.wait_ge(z_ready, past(b))
                af(scaled[:, 0, :, :], pC_y[:, :, 0:D], ACT.Copy).then_inc(scaled_ready, 1)
                for i, factor in ((1, amp), (2, att)):
                    for h in range(NH):
                        af(scaled[:, i, h, :], pC_y[:, h, i * D:(i + 1) * D], ACT.Identity, scale=factor[:, par, h:h + 1])\
                            .then_inc(scaled_ready, 1)

            def sd_2(b):
                act.wait_ge(mv2_ready, 2 * b + 2)
                act.wait_ge(rs2_ready, past(b))
                af(sd2[:, :], mv2[:, :, 1], ACT.Sqrt, bias=epscol[:, 0:1]).then_inc(sd2_ready, 1)

            def norm2(b, par, k):
                act.wait_ge(nb2_ready, b + 1)
                act.wait_ge(out_stored[par], past(16 * k))
                for h in range(NH):
                    af(zo[:, par, h, :], z[:, h, :], ACT.Identity, bias=nb2[:, h:h + 1], scale=rs2[:, h:h + 1])\
                        .then_inc(zo_ready, 1)

            def store(b, par, k, graph=None):
                graph = b if graph is None else graph
                act.wait_ge(zo_ready, 2 * b + 2)
                act.dma_start(out_v[:, bass.ds(2 * graph, 2), :], zo[:, par, :, :]).then_inc(out_stored[par], 16)

            def gcn(b, par, k):
                copy_adjT(b, par)
                copy_agg0(b)
                relu(b, h1_done, h1_relu)
                relu(b, h2_done, h2_relu)
                relu(b, h3_done, h3_relu)
                if first(b):
                    constants()

            def sums(b, par, k, r=None):
                scale_y(b)
                sd_1(b)
                norm1(b, par)
                copy_x1T(b, par)
                copy_code(b, par, r)
                v_parts(b, par)
                high_part(b, par)

            def spread(b, par):
                scale_q(b)
                scale_u(b)
                scale_uc(b)
                std(b, par)
                log_deg(b, 1, par)

            def post(b, par, k, graph=None):
                copy_msT(b)
                scale_post(b, par)
                sd_2(b)
                norm2(b, par, k)
                store(b, par, k, graph)

            def turn(ga, gn, gb, gc):
                b, bpar, _ = gb or (None, None, None)
                if gn:
                    scale_y(gn[0])
                if gb:
                    scale_q(b)
                    start_best(b, bpar)
                if ga:
                    copy_adjT(*ga[:2])
                if gn:
                    sd_1(gn[0])
                if gc:
                    copy_msT(gc[0])
                if gb:
                    scale_u(b)
                if bpar == 1:
                    log_deg(b, 2, slice(0, 2))
                if ga:
                    copy_agg0(ga[0])
                if gn:
                    norm1(*gn[:2])
                if gb:
                    scale_uc(b)
                if ga:
                    relu(ga[0], h1_done, h1_relu)
                if gn:
                    copy_x1T(*gn[:2])
                if gc:
                    scale_post(*gc[:2])
                if gn:
                    v_parts(*gn[:2])
                if gb:
                    std(b, bpar)
                if gc:
                    sd_2(gc[0])
                if ga:
                    relu(ga[0], h2_done, h2_relu)
                if gn:
                    copy_code(*gn[:2])
                if gc:
                    norm2(*gc)
                if gn:
                    high_part(*gn[:2])
                if ga:
                    relu(ga[0], h3_done, h3_relu)
                if gc:
                    store(*gc)

            def one_round(v, par, k, graph, r):
                act.wait_ge(rounds_set, ROUNDS + 3)
                gcn(v, par, k)
                sums(v, par, k, r)
                start_best(v, par)
                spread(v, par)
                copy_msT(v)
                scale_post(v, par)
                sd_2(v)
                norm2(v, par, k)
                act.wait_ge(out_stored[1 - par], 16 * (k + par))
                store(v, par, k, graph)

            every_turn(act, gcn, post, turn)
            every_round(act, one_round)

        @block.vector
        def _(dve):
            v = nc.vector
            v.memset(xa[:, 0, :, D:D + 1], 1.0).then_inc(consts_set, 1)
            v.memset(xa[:, 1, :, D:D + 1], 1.0).then_inc(consts_set, 1)
            v.memset(onerow[:, :], 1.0).then_inc(consts_set, 1)
            v.memset(Wuv[D:D + 2, :, :], 0.0).then_inc(rows_filled, 1)
            v.memset(Wum[D:D + 2, :, :], -BIG).then_inc(rows_filled, 1)
            v.memset(x1[:, :, :, :], 1.0).then_inc(consts_set, 1)
            v.memset(vv[:, :, 2 * D:2 * D + 1], 1.0).then_inc(consts_set, 1)
            v.memset(epscol[:, :], EPS).then_inc(consts_set, 1)
            v.memset(lo_scale[:, :], LO).then_inc(consts_set, 1)
            v.memset(most[:, :, :], 0.0).then_inc(consts_set, 1)
            v.memset(ones[:, :], 1.0).then_inc(consts_set, 1)
            v.memset(ones64[:, :], 1.0).then_inc(consts_set, 1)
            dve.wait_ge(consts_set, N_CONST)
            dve.wait_ge(rows_filled, 2)

            def constants():
                dve.wait_ge(w_loaded, 16 * N_W)
                v.tensor_tensor(Wsq[:, :], Wuv[0:D, 1, :], Wuv[0:D, 1, :], ALU.mult).then_inc(wsq_ready, 1)
                v.tensor_copy(Wum[0:D, 0, :], Wuv[0:D, 0, :]).then_inc(wcopies_ready, 1)
                v.tensor_scalar(Wum[0:D, 1, :], Wuv[0:D, 0, :], -1.0, None, ALU.mult).then_inc(wcopies_ready, 1)
                v.tensor_tensor(Wuv[0:D, 2, :], Wuv[0:D, 2, :], ident[0:D, 0:D], ALU.add).then_inc(wx_ready, 1)
                v.tensor_scalar(Wmx[D:P, :, :], Wmx[D:P, :, :], -1.0, None, ALU.mult).then_inc(wpost_neg, 1)
                dve.wait_ge(mask_turned, 1)
                v.tensor_copy(nmask[:, :], pC[:, 0:NH * B]).then_inc(nmask_ready, 1)
                dve.wait_ge(shift_ready, 1)
                row = slice(D, D + 1)
                v.tensor_tensor(Wum[row, 0, :], Wuv[row, 0, :], shift[row, :], ALU.subtract).then_inc(wrows_ready, 1)
                v.scalar_tensor_tensor(out=Wum[row, 1, :], in0=Wuv[row, 0, :], scalar=-1.0, in1=shift[row, :],
                                       op0=ALU.mult, op1=ALU.subtract).then_inc(wrows_ready, 1)
                dve.wait_ge(nmask_ready, 1)

            def get_mask(b, par):
                dve.wait_ge(adjT_copied, b + 1)
                dve.wait_ge(nums_done, past(b - 1))
                dve.wait_ge(counts_done, past(b - 1))
                v.tensor_scalar(maskT[:, par, :, :].rearrange("p h n -> p (h n)"),
                                adjT[:, par, :, :].rearrange("p h n -> p (h n)"), 0.0, None, ALU.is_gt)\
                    .then_inc(maskT_ready, 1)

            def add_bias(b, layer, done, ready):
                dve.wait_ge(done, b + 1)
                v.tensor_tensor(msg[:, :, :], pG[:, 0:N].rearrange("p (h c) -> p h c", h=NH),
                                bias[:, None, layer, :].to_broadcast([P, NH, H]), ALU.add).then_inc(ready, 1)

            def count(b, par):
                dve.wait_ge(counts_done, b + 1)
                v.tensor_reduce(total[:, :], pT[:, 0:NH * NH].rearrange("p (a b) -> p a b", a=NH), AX, ALU.add)\
                    .then_inc(total_ready, 1)
                dve.wait_ge(most_ready, past(b))
                v.tensor_tensor(most[:, :, :], pT[:, 0:NH * NH].rearrange("p (a b) -> p a b", a=NH), most[:, :, :],
                                ALU.max).then_inc(most_ready, 1)
                dve.wait_ge(total_ready, b + 1)
                dve.wait_ge(x1_turned, past(b - 1))
                v.tensor_scalar(x1[:, par, :, D + 1], total[:, :], 0.0, None, ALU.is_equal).then_inc(iso_ready, 1)

            def stats(b, src, ready, st, st_ready, mv, mv_ready):
                dve.wait_ge(ready, b + 1)
                for h in range(NH):
                    v.bn_stats(st[:, h, :], src[:, h, :]).then_inc(st_ready, 1)
                dve.wait_ge(st_ready, 2 * b + 2)
                v.memset(gate[:, :], 0.0)
                for h in range(NH):
                    v.bn_aggr(mv[:, h, :], st[:, h, :]).then_inc(mv_ready, 1)

            def graph_mask(b, graph=None):
                graph = b if graph is None else graph
                dve.wait_ge(y0_ready, past(2 * b))
                v.tensor_scalar(gmask[:, :], nmask[:, bass.ds(2 * graph, 2)], 1.0, None, ALU.mult)\
                    .then_inc(gmask_ready, 1)

            def factors(b, mv, sd, sd_ready, rs, rs_ready, nb, nb_ready, read):
                dve.wait_ge(sd_ready, b + 1)
                dve.wait_ge(read, past(2 * b))
                v.reciprocal(rs[:, :], sd[:, :]).then_inc(rs_ready, 1)
                dve.wait_ge(rs_ready, b + 1)
                v.scalar_tensor_tensor(out=nb[:, :], in0=mv[:, :, 0], scalar=-1.0, in1=rs[:, :], op0=ALU.mult,
                                       op1=ALU.mult).then_inc(nb_ready, 1)

            def factors1(b):
                factors(b, mv1, sd1, sd1_ready, rs1, rs1_ready, nb1, nb1_ready, x1_ready)

            def factors2(b):
                factors(b, mv2, sd2, sd2_ready, rs2, rs2_ready, nb2, nb2_ready, zo_ready)

            def make_onehot(b, par, t):
                dve.wait_ge(slot_done, past(PAIRS * (b - 1) + t + 1))
                dve.wait_ge(code_ready, b + 1)
                for j in range(2):
                    v.tensor_scalar(onehot[:, t, :, j, :], code[:, par, :, :], float(RANK0 + 2 * t + j + 1), HALF,
                                    ALU.is_equal, ALU.mult).then_inc(onehot_ready, 1)

            def update_best(b, par, t):
                dve.wait_ge(slot_done, PAIRS * b + t + 1)
                if t == 1:
                    dve.wait_ge(best_started, b + 1)
                else:
                    dve.wait_ge(best_updated, (PAIRS - 1) * b + t - 1)
                bv = best[:, :, :, :].rearrange("p h j n -> p (h j n)")
                v.tensor_tensor(bv, pS[(par * PAIRS + t) % 2][:, :], bv, ALU.max).then_inc(best_updated, 1)

            def degree(b, par):
                dve.wait_ge(sums_done, b + 1)
                dve.wait_ge(lg_ready, past(b - 1))
                v.tensor_copy(deg[:, par, :], pU_s[:, :, 2 * D]).then_inc(deg_copied, 1)
                dve.wait_ge(deg_copied, b + 1)
                v.tensor_scalar(degs[:, :], deg[:, par, :], 1.0, None, ALU.max).then_inc(degs_ready, 1)

            def inverse_degree(b):
                dve.wait_ge(degs_ready, b + 1)
                dve.wait_ge(q_ready, past(2 * b))
                v.reciprocal(rdeg[:, :], degs[:, :]).then_inc(rdeg_ready, 1)

            def ratios(b, par):
                dve.wait_ge(rdeg_ready, b + 1)
                dve.wait_ge(ru_ready, past(2 * b))
                v.tensor_tensor(ratio[:, :], deg[:, par, :], rdeg[:, :], ALU.mult).then_inc(ratio_ready, 1)
                dve.wait_ge(ratio_ready, b + 1)
                dve.wait_ge(su_ready, past(2 * b))
                v.tensor_scalar(slack[:, :], ratio[:, :], -1.0, 1.0, ALU.mult, ALU.add).then_inc(slack_ready, 1)

            def scalers(b, graphs, which):
                dve.wait_ge(lg_ready, b + 1)
                dve.wait_ge(scaled_ready, past(5 * (b - 1)))
                v.tensor_scalar(lgs[:, which, :], lg[:, which, :], EPS, None, ALU.max).then_inc(lgs_ready, graphs)
                v.tensor_scalar(amp[:, which, :], lg[:, which, :], 1.0 / AVG_D_LOG, None, ALU.mult)\
                    .then_inc(amp_ready, graphs)
                dve.wait_ge(lgs_ready, b + 1)
                v.reciprocal(att0[:, which, :], lgs[:, which, :]).then_inc(att0_ready, graphs)
                dve.wait_ge(att0_ready, b + 1)
                v.tensor_scalar(att[:, which, :], att0[:, which, :], AVG_D_LOG, None, ALU.mult).then_inc(att_ready, graphs)

            def fold_best(b):
                dve.wait_ge(best_updated, (PAIRS - 1) * (b + 1))
                v.tensor_tensor(best2[:, :, :], best[:, 0, :, :], best[:, 1, :, :], ALU.max).then_inc(best2_ready, 1)
                dve.wait_ge(best2_ready, b + 1)
                dve.wait_ge(mx_ready, past(b))
                v.tensor_tensor(best1[:, :], best2[:, 0, :], best2[:, 1, :], ALU.max).then_inc(best1_ready, 1)

            def carry_best(v, r):
                dve.wait_ge(best1_ready, v + 1)
                dve.wait_ge(mx_ready, past(v))
                nc.vector.scalar_tensor_tensor(out=carry[:, :], in0=carry[:, :], scalar=keep[:, bass.ds(r, 1)],
                                               in1=best1[:, :], op0=ALU.mult, op1=ALU.max)\
                    .then_inc(carry_ready, 1)

            def add_u(b, top=best1):
                dve.wait_ge(ms_turned, b + 1)
                dve.wait_ge(best1_ready, b + 1)
                dve.wait_ge(post_done, past(b))
                v.scalar_tensor_tensor(out=mx[:, :], in0=top[:, :], scalar=1.0 / HALF, in1=pC[:, N:2 * N],
                                       op0=ALU.mult, op1=ALU.add).then_inc(mx_ready, 1)

            def stats2(b):
                stats(b, z, z_ready, st2, st2_ready, mv2, mv2_ready)

            def stats1(b):
                stats(b, y, y_ready, st1, st1_ready, mv1, mv1_ready)

            def gcn(b, par, k, graph=None):
                get_mask(b, par)
                count(b, par)
                add_bias(b, 0, msg1_done, msg1_ready)
                add_bias(b, 1, msg2_done, msg2_ready)
                if first(b):
                    constants()
                graph_mask(b, graph)

            def sums(b, par, k):
                stats1(b)
                factors1(b)

            def before(b, par, k):
                for t in range(2):
                    make_onehot(b, par, t)

            def slots(b, par):
                degree(b, par)
                inverse_degree(b)
                ratios(b, par)
                scalers(b, 1, par)
                for t in range(2, PAIRS):
                    make_onehot(b, par, t)
                for t in range(1, PAIRS):
                    update_best(b, par, t)
                fold_best(b)

            def post(b, par, k):
                add_u(b)
                stats2(b)
                factors2(b)

            def turn(ga, gn, gb, gc):
                b, bpar, _ = gb or (None, None, None)
                if gb:
                    degree(b, bpar)
                    inverse_degree(b)
                    make_onehot(b, bpar, 2)
                if gc:
                    add_u(gc[0])
                if gn:
                    stats1(gn[0])
                if gb:
                    ratios(b, bpar)
                    make_onehot(b, bpar, 3)
                    make_onehot(b, bpar, 4)
                    update_best(b, bpar, 1)
                if gn:
                    factors1(gn[0])
                if ga:
                    get_mask(*ga[:2])
                if gb:
                    update_best(b, bpar, 2)
                    make_onehot(b, bpar, 5)
                if bpar == 1:
                    scalers(b, 2, slice(0, 2))
                if gb:
                    update_best(b, bpar, 3)
                if ga:
                    count(*ga[:2])
                    graph_mask(ga[0])
                if gb:
                    update_best(b, bpar, 4)
                if ga:
                    add_bias(ga[0], 0, msg1_done, msg1_ready)
                if gb:
                    make_onehot(b, bpar, 6)
                if gc:
                    stats2(gc[0])
                if gb:
                    update_best(b, bpar, 5)
                if gc:
                    factors2(gc[0])
                if gn:
                    make_onehot(gn[0], gn[1], 0)
                if ga:
                    add_bias(ga[0], 1, msg2_done, msg2_ready)
                if gn:
                    make_onehot(gn[0], gn[1], 1)
                if gb:
                    update_best(b, bpar, 6)
                    fold_best(b)

            def make_flag():
                dve.wait_ge(most_ready, B)
                v.tensor_reduce(worst[:, :], most[:, :, :].rearrange("p a b -> p (a b)"), AX, ALU.max)\
                    .then_inc(worst_ready, 1)
                dve.wait_ge(worst_ready, 1)
                v.tensor_scalar(over[:, :], worst[:, :], float(SLOTS), None, ALU.is_gt)\
                    .then_inc(over_ready, 1)
                dve.wait_ge(over_summed, 1)
                v.tensor_copy(flag[0:1, 0:1], pT[0:1, 0:1]).then_inc(flag_ready, 1)

            def one_round(n, par, k, graph, r):
                gcn(n, par, k, graph)
                sums(n, par, k)
                before(n, par, k)
                slots(n, par)
                carry_best(n, r)
                dve.wait_ge(carry_ready, n - B + 1)
                add_u(n, carry)
                stats2(n)
                factors2(n)

            every_turn(dve, gcn, post, turn, make_flag)
            dve.wait_ge(flag_ready, 1)
            with dve.If(over_flag(dve) > 0):
                for r in range(ROUNDS):
                    v.memset(back[:, r:r + 1], float(-SLOTS * r)).then_inc(rounds_set, 1)
                v.memset(carry[:, :], 0.0).then_inc(rounds_set, 1)
                v.memset(keep[:, 0:1], 0.0).then_inc(rounds_set, 1)
                v.memset(keep[:, 1:ROUNDS], 1.0).then_inc(rounds_set, 1)
                dve.wait_ge(rounds_set, ROUNDS + 3)
            every_round(dve, one_round)

        @block.gpsimd
        def _(pool):
            g = nc.gpsimd
            cs_ = consts_set
            g.memset(ident[:, :], 0.0).then_inc(poolstep, 1)
            g.memset(tri[:, :], 1.0).then_inc(poolstep, 1)
            pool.wait_ge(poolstep, 2)
            g.affine_select(out=ident[:, :], in_=ident[:, :], compare_op=ALU.not_equal, fill=1.0, base=0,
                            pattern=[[-1, P]], channel_multiplier=1).then_inc(consts_set, 1)
            g.affine_select(out=tri[:, :], in_=tri[:, :], compare_op=ALU.is_ge, fill=0.0, base=0,
                            pattern=[[1, P]], channel_multiplier=-1).then_inc(poolstep, 1)
            pool.wait_ge(poolstep, 3)
            g.affine_select(out=tri[:, :], in_=tri[:, :], compare_op=ALU.not_equal, fill=float(RANK0 + 1), base=0,
                            pattern=[[-1, P]], channel_multiplier=1).then_inc(consts_set, 1)

            def shifted(b):
                if first(b):
                    pool.wait_ge(shift_ready, 1)
                pool.wait_ge(v_copied, b + 1)
                pool.wait_ge(vhi_ready, past(b))
                pool.wait_ge(vres_ready, past(b))
                sh = shift[:, None, :].to_broadcast([P, NH, D])
                g.tensor_tensor(vfull[:, :, 0:D], vv[:, :, 0:D], sh, ALU.add).then_inc(vfull_ready, 1)
                g.tensor_tensor(vfull[:, :, D:2 * D], sh, vv[:, :, 0:D], ALU.subtract).then_inc(vfull_ready, 1)

            def low(b, par):
                pool.wait_ge(vhi_ready, b + 1)
                pool.wait_ge(vfull_ready, 2 * b + 2)
                pool.wait_ge(vlo_ready, past(b))
                g.tensor_tensor(vres[:, :, :], vfull[:, :, :], vhi[:, par, :, :], ALU.subtract).then_inc(vres_ready, 1)
                pool.wait_ge(vres_ready, b + 1)
                pool.wait_ge(slot_done, past(PAIRS * (b - 1)))
                g.tensor_tensor(vlo[:, par, :, :], vres[:, :, :], lo_scale[:, None, :].to_broadcast([P, NH, 2 * D]),
                                ALU.mult).then_inc(vlo_ready, 1)

            def add_residual(b, par):
                pool.wait_ge(y0_ready, 2 * b + 2)
                pool.wait_ge(x1_ready, past(2 * b))
                g.tensor_tensor(y[:, :, :], y0[:, :, :], xa[:, par, :, 0:D], ALU.add).then_inc(y_ready, 1)

            def square_q1(b):
                pool.wait_ge(q_ready, 2 * b + 2)
                g.tensor_tensor(q1sq[:, :, :], q[:, :, 0:D], q[:, :, 0:D], ALU.mult).then_inc(q1sq_ready, 1)
                pool.wait_ge(q1sq_ready, b + 1)
                pool.wait_ge(var0_ready, past(b))
                g.tensor_tensor(vb[:, :, :], q[:, :, D:2 * D], q1sq[:, :, :], ALU.subtract).then_inc(vb_ready, 1)

            def mean_of(b, par):
                pool.wait_ge(ru_ready, 2 * b + 2)
                pool.wait_ge(ms_turned, past(b - 1))
                g.tensor_tensor(ms[:, par, :, 0:D], ru[:, :, :], q[:, :, 0:D], ALU.add).then_inc(mean_ready, 1)
                pool.wait_ge(mean_ready, b + 1)
                g.tensor_tensor(cs[:, :, :], ms[:, par, :, 0:D], q[:, :, 0:D], ALU.add).then_inc(cs_ready, 1)
                pool.wait_ge(cs_ready, b + 1)
                pool.wait_ge(su_ready, past(2 * b))
                g.tensor_tensor(uc[:, :, :], us[:, :, :], cs[:, :, :], ALU.mult).then_inc(uc_ready, 1)

            def variance(b):
                pool.wait_ge(su_ready, 2 * b + 2)
                pool.wait_ge(vb_ready, b + 1)
                pool.wait_ge(var1_ready, past(b))
                g.tensor_tensor(var0[:, :, :], su[:, :, :], vb[:, :, :], ALU.add).then_inc(var0_ready, 1)

            def combine(b, par):
                pool.wait_ge(scaled_ready, 5 * b + 5)
                g.tensor_tensor(za[:, :, :], scaled[:, 0, :, :], scaled[:, 1, :, :], ALU.add).then_inc(za_ready, 1)
                pool.wait_ge(xw_copied, b + 1)
                g.tensor_tensor(zb[:, :, :], scaled[:, 2, :, :], xw[:, par, :, :], ALU.add).then_inc(zb_ready, 1)
                pool.wait_ge(za_ready, b + 1)
                pool.wait_ge(zb_ready, b + 1)
                pool.wait_ge(zo_ready, past(2 * b))
                g.tensor_tensor(z[:, :, :], za[:, :, :], zb[:, :, :], ALU.add).then_inc(z_ready, 1)

            def gcn(b, par, k):
                pass

            def sums(b, par, k):
                add_residual(b, par)
                shifted(b)
                low(b, par)

            def spread(b, par):
                square_q1(b)
                mean_of(b, par)
                variance(b)

            def post(b, par, k):
                combine(b, par)

            def turn(ga, gn, gb, gc):
                if gn:
                    add_residual(*gn[:2])
                if gb:
                    spread(*gb[:2])
                if gc:
                    combine(*gc[:2])
                if gn:
                    shifted(gn[0])
                    low(*gn[:2])

            def one_round(v, par, k, graph, r):
                sums(v, par, k)
                spread(v, par)
                post(v, par, k)

            every_turn(pool, gcn, post, turn)
            every_round(pool, one_round)


_INS = ['x', 'adj', 'nodemask', 'L0_gnn_W0', 'L0_gnn_b0', 'L0_gnn_W1', 'L0_gnn_b1', 'L0_gnn_W2', 'L0_gnn_b2',
        'L0_gnn_Wout', 'L0_gnn_bout', 'L1_gnn_W_pre', 'L1_gnn_b_pre', 'L1_gnn_W_post', 'L1_gnn_b_post']


def kernel(**inputs):
    import numpy as _np
    import concourse.bacc as _bacc
    from concourse import mybir as _mybir
    from concourse.bass_utils import run_bass_kernel_spmd as _run

    nc = _bacc.Bacc("TRN2", target_bir_lowering=False, num_devices=1)
    arrays, args = {}, []
    for name in _INS:
        a = _np.ascontiguousarray(inputs[name])
        arrays[f"in_{name}_dram"] = a
        args.append(nc.dram_tensor(f"in_{name}_dram", a.shape, _mybir.dt.from_np(a.dtype), kind="ExternalInput").ap())
    shape = _np.asarray(inputs["x"]).shape
    args.append(nc.dram_tensor("out_dram", shape, _mybir.dt.float32, kind="ExternalOutput").ap())
    gcn_pna_program(nc, *args)
    r = _run(nc, [arrays], core_ids=[0])
    return r.results[0]["out_dram"]
```
